# Optimizing a Trainium2 kernel written in Bass

```python
import numpy as np
import jax
import jax.numpy as jnp

def _softmax(x, axis=-1):
    return jax.nn.softmax(x, axis=axis)

def _gelu(x):
    return jax.nn.gelu(x, approximate=True)

def _silu(x):
    return jax.nn.silu(x)

def _sigmoid(x):
    return jax.nn.sigmoid(x)

def _layernorm(x, axis=-1, eps=1e-05):
    m = jnp.mean(x, axis=axis, keepdims=True)
    v = jnp.var(x, axis=axis, keepdims=True)
    return (x - m) / jnp.sqrt(v + eps)

def _scatter_add(tgt, idx, src, axis=0):
    return tgt.at[idx].add(src)

def _segment_sum(src, seg, n):
    return jax.ops.segment_sum(src, seg, n)
kernel_name = 'mk_gnn_resnorm_d4_gnn_r8_202262'

def setup_inputs(seed: int=0):
    np.random.seed(seed)
    _w = jnp.asarray

    def _rec_inputs():
        import jax
        import jax.numpy as jnp
        _gk = jax.random.key(seed)
        x = -0.000202 + 1 * jax.random.normal(jax.random.fold_in(_gk, 1), (12500, 128), jnp.float32)
        _s = jax.random.randint(jax.random.fold_in(_gk, 2), (100000,), 0, 12500, jnp.int32)
        _d = jax.random.randint(jax.random.fold_in(_gk, 3), (100000,), 0, 12500, jnp.int32)
        _loop = jnp.arange(12500, dtype=jnp.int32)
        src = jnp.concatenate([_s, _d, _loop])
        dst = jnp.concatenate([_d, _s, _loop])
        _o = jnp.argsort(dst, stable=True)
        src = src[_o]
        dst = dst[_o]
        edge_attr_50 = 0.000152336 + 1.00009 * jax.random.normal(jax.random.fold_in(_gk, 11), (212500, 50), jnp.float32)
        edge_attr_8 = jax.random.uniform(jax.random.fold_in(_gk, 12), (212500, 8), jnp.float32, 0.0, 1)
        edge_weight = jax.random.uniform(jax.random.fold_in(_gk, 14), (212500,), jnp.float32, 0.0, 9.99998)
        return (x, src, dst, edge_attr_50, edge_attr_8, edge_weight)
    x, src, dst, edge_attr_50, edge_attr_8, edge_weight = _rec_inputs()

    def _L0_gnn_setup():
        import jax, jax.numpy as jnp
        import numpy as np
        N_NODES = 6250
        N_EDGES = 100000
        IN_DIM = 128
        NUM_HEADS = 8
        HEAD_DIM = 16
        NEG_SLOPE = 0.2
        key = jax.random.key(seed)
        k1, k2, k3, k4, k5 = jax.random.split(key, 5)
        x = jax.random.normal(k1, (N_NODES, IN_DIM), dtype=jnp.float32)
        edge_indices = jax.random.randint(k2, (2, N_EDGES), 0, N_NODES, dtype=jnp.int32)
        W = jax.random.normal(k3, (IN_DIM, NUM_HEADS * HEAD_DIM), dtype=jnp.float32) * (1.0 / np.sqrt(IN_DIM))
        src_attn = jax.random.normal(k4, (1, NUM_HEADS, HEAD_DIM), dtype=jnp.float32) * (1.0 / np.sqrt(2 * HEAD_DIM))
        dst_attn = jax.random.normal(k5, (1, NUM_HEADS, HEAD_DIM), dtype=jnp.float32) * (1.0 / np.sqrt(2 * HEAD_DIM))
        return {'x': x, 'edge_indices': edge_indices, 'W': W, 'src_attn': src_attn, 'dst_attn': dst_attn}
    _L0_gnn_all = _L0_gnn_setup()
    _L0_gnn_in = {k: v for k, v in _L0_gnn_all.items() if k in ('W', 'src_attn', 'dst_attn')}
    del _L0_gnn_all

    def _L1_gnn_setup():
        import jax, jax.numpy as jnp
        import numpy as np
        N_NODES = 6250
        N_EDGES = 100000
        DIM = 128
        HEADS = 8
        HEAD_DIM = DIM // HEADS
        key = jax.random.key(seed)
        ks = jax.random.split(key, 12)
        s = 1.0 / np.sqrt(DIM)
        return {'x': jax.random.normal(ks[0], (N_NODES, DIM), jnp.float32), 'edge_index': jax.random.randint(ks[1], (2, N_EDGES), 0, N_NODES, jnp.int32), 'edge_weights': jax.random.uniform(ks[2], (N_EDGES, HEADS), jnp.float32), 'Wq': jax.random.normal(ks[3], (DIM, DIM), jnp.float32) * s, 'bq': jnp.zeros((DIM,), jnp.float32), 'Wk': jax.random.normal(ks[4], (DIM, DIM), jnp.float32) * s, 'bk': jnp.zeros((DIM,), jnp.float32), 'Wv': jax.random.normal(ks[5], (DIM, DIM), jnp.float32) * s, 'bv': jnp.zeros((DIM,), jnp.float32), 'Wo': jax.random.normal(ks[6], (DIM, DIM), jnp.float32) * s, 'bo': jnp.zeros((DIM,), jnp.float32), 'gamma': jnp.ones((DIM,), jnp.float32), 'beta': jnp.zeros((DIM,), jnp.float32)}
    _L1_gnn_all = _L1_gnn_setup()
    _L1_gnn_in = {k: v for k, v in _L1_gnn_all.items() if k in ('Wq', 'bq', 'Wk', 'bk', 'Wv', 'bv', 'Wo', 'bo', 'gamma', 'beta')}
    del _L1_gnn_all

    def _L2_gnn_setup():
        import jax, jax.numpy as jnp
        import numpy as np
        N = 6250
        E = 100000
        IN_C = 128
        HID = 16
        HEADS = 8
        NEG_SLOPE = 0.2

        def _gatv2_layer(x, src, dst, Wl, Wr, att, bias):
            n = x.shape[0]
            xl = (x @ Wl).reshape(n, HEADS, HID)
            xr = (x @ Wr).reshape(n, HEADS, HID)
            e = jax.nn.leaky_relu(xl[src] + xr[dst], NEG_SLOPE)
            score = jnp.einsum('ehc,hc->eh', e, att)
            m = jax.ops.segment_max(score, dst, num_segments=n)
            alpha = jnp.exp(score - m[dst])
            denom = jax.ops.segment_sum(alpha, dst, num_segments=n)
            alpha = alpha / denom[dst]
            out = jax.ops.segment_sum(alpha[:, :, None] * xl[src], dst, num_segments=n)
            return out.reshape(n, HEADS * HID) + bias
        key = jax.random.key(seed)
        k1, k2, k3, k4, k5, k6 = jax.random.split(key, 6)
        x = jax.random.normal(k1, (N, IN_C), dtype=jnp.float32)
        edge_index = jax.random.randint(k2, (2, E), 0, N, dtype=jnp.int64)
        s = 1.0 / np.sqrt(IN_C)
        Wl = jax.random.normal(k3, (IN_C, HEADS * HID), dtype=jnp.float32) * s
        Wr = jax.random.normal(k4, (IN_C, HEADS * HID), dtype=jnp.float32) * s
        att = jax.random.normal(k5, (HEADS, HID), dtype=jnp.float32) * (1.0 / np.sqrt(HID))
        bias = jax.random.normal(k6, (HEADS * HID,), dtype=jnp.float32) * 0.01
        return {'x': x, 'edge_index': edge_index, 'Wl': Wl, 'Wr': Wr, 'att': att, 'bias': bias}
    _L2_gnn_all = _L2_gnn_setup()
    _L2_gnn_in = {k: v for k, v in _L2_gnn_all.items() if k in ('Wl', 'Wr', 'att', 'bias')}
    del _L2_gnn_all

    def _L3_gnn_setup():
        import jax, jax.numpy as jnp
        import numpy as np
        N_NODES = 5000
        N_EDGES = 80000
        HIDDEN = 128
        NUM_RBF = 50
        CUTOFF = 10.0
        key = jax.random.key(seed)
        ks = jax.random.split(key, 8)
        s = 1.0 / np.sqrt(HIDDEN)
        sf = 1.0 / np.sqrt(NUM_RBF)
        return {'x': jax.random.normal(ks[0], (N_NODES, HIDDEN), dtype=jnp.float32), 'edge_index': jax.random.randint(ks[1], (2, N_EDGES), 0, N_NODES, dtype=jnp.int64), 'edge_weight': jax.random.uniform(ks[2], (N_EDGES,), dtype=jnp.float32) * CUTOFF, 'edge_attr': jax.random.normal(ks[3], (N_EDGES, NUM_RBF), dtype=jnp.float32), 'W_f1': jax.random.normal(ks[4], (NUM_RBF, HIDDEN), dtype=jnp.float32) * sf, 'b_f1': jnp.zeros((HIDDEN,), dtype=jnp.float32), 'W_f2': jax.random.normal(ks[5], (HIDDEN, HIDDEN), dtype=jnp.float32) * s, 'b_f2': jnp.zeros((HIDDEN,), dtype=jnp.float32), 'W_in': jax.random.normal(ks[6], (HIDDEN, HIDDEN), dtype=jnp.float32) * s, 'W_out': jax.random.normal(ks[7], (HIDDEN, HIDDEN), dtype=jnp.float32) * s, 'b_out': jnp.zeros((HIDDEN,), dtype=jnp.float32), 'W_lin': jax.random.normal(jax.random.fold_in(key, 7), (HIDDEN, HIDDEN), dtype=jnp.float32) * s, 'b_lin': jnp.zeros((HIDDEN,), dtype=jnp.float32)}
    _L3_gnn_all = _L3_gnn_setup()
    _L3_gnn_in = {k: v for k, v in _L3_gnn_all.items() if k in ('W_f1', 'b_f1', 'W_f2', 'b_f2', 'W_in', 'W_out', 'b_out', 'W_lin', 'b_lin')}
    del _L3_gnn_all
    return {'x': x, 'src': src, 'dst': dst, 'edge_attr_50': edge_attr_50, 'edge_attr_8': edge_attr_8, 'edge_weight': edge_weight, 'L0_gnn_W': _L0_gnn_in['W'], 'L0_gnn_src_attn': _L0_gnn_in['src_attn'], 'L0_gnn_dst_attn': _L0_gnn_in['dst_attn'], 'L1_gnn_Wq': _L1_gnn_in['Wq'], 'L1_gnn_bq': _L1_gnn_in['bq'], 'L1_gnn_Wk': _L1_gnn_in['Wk'], 'L1_gnn_bk': _L1_gnn_in['bk'], 'L1_gnn_Wv': _L1_gnn_in['Wv'], 'L1_gnn_bv': _L1_gnn_in['bv'], 'L1_gnn_Wo': _L1_gnn_in['Wo'], 'L1_gnn_bo': _L1_gnn_in['bo'], 'L1_gnn_gamma': _L1_gnn_in['gamma'], 'L1_gnn_beta': _L1_gnn_in['beta'], 'L2_gnn_Wl': _L2_gnn_in['Wl'], 'L2_gnn_Wr': _L2_gnn_in['Wr'], 'L2_gnn_att': _L2_gnn_in['att'], 'L2_gnn_bias': _L2_gnn_in['bias'], 'L3_gnn_W_f1': _L3_gnn_in['W_f1'], 'L3_gnn_b_f1': _L3_gnn_in['b_f1'], 'L3_gnn_W_f2': _L3_gnn_in['W_f2'], 'L3_gnn_b_f2': _L3_gnn_in['b_f2'], 'L3_gnn_W_in': _L3_gnn_in['W_in'], 'L3_gnn_W_out': _L3_gnn_in['W_out'], 'L3_gnn_b_out': _L3_gnn_in['b_out'], 'L3_gnn_W_lin': _L3_gnn_in['W_lin'], 'L3_gnn_b_lin': _L3_gnn_in['b_lin']}

def reference(x, src, dst, edge_attr_50, edge_attr_8, edge_weight, L0_gnn_W, L0_gnn_src_attn, L0_gnn_dst_attn, L1_gnn_Wq, L1_gnn_bq, L1_gnn_Wk, L1_gnn_bk, L1_gnn_Wv, L1_gnn_bv, L1_gnn_Wo, L1_gnn_bo, L1_gnn_gamma, L1_gnn_beta, L2_gnn_Wl, L2_gnn_Wr, L2_gnn_att, L2_gnn_bias, L3_gnn_W_f1, L3_gnn_b_f1, L3_gnn_W_f2, L3_gnn_b_f2, L3_gnn_W_in, L3_gnn_W_out, L3_gnn_b_out, L3_gnn_W_lin, L3_gnn_b_lin):
    import jax
    import jax.numpy as jnp

    def _L0_gnn_ref(x, edge_indices, W, src_attn, dst_attn):
        import jax, jax.numpy as jnp
        import numpy as np
        N_NODES = 6250
        N_EDGES = 100000
        IN_DIM = 128
        NUM_HEADS = 8
        HEAD_DIM = 16
        NEG_SLOPE = 0.2
        n = x.shape[0]
        src, dst = (edge_indices[0], edge_indices[1])
        h = (x @ W).reshape(n, NUM_HEADS, HEAD_DIM)
        s_src = (h * src_attn).sum(-1)
        s_dst = (h * dst_attn).sum(-1)
        coef = s_src[src] + s_dst[dst]
        coef = jnp.where(coef >= 0, coef, NEG_SLOPE * coef)
        m = jax.ops.segment_max(coef, dst, num_segments=n)
        v = jnp.exp(coef - m[dst])
        s = jax.ops.segment_sum(v, dst, num_segments=n)
        v = v / s[dst]
        msgs = h[dst] * v[:, :, None]
        out = jax.ops.segment_sum(msgs, src, num_segments=n)
        return out.reshape(n, NUM_HEADS * HEAD_DIM)

    def _L1_gnn_ref(x, edge_index, edge_weights, Wq, bq, Wk, bk, Wv, bv, Wo, bo, gamma, beta):
        import jax, jax.numpy as jnp
        import numpy as np
        N_NODES = 6250
        N_EDGES = 100000
        DIM = 128
        HEADS = 8
        HEAD_DIM = DIM // HEADS
        n = x.shape[0]
        origin, dest = (edge_index[0], edge_index[1])
        scale = HEAD_DIM ** (-0.5)
        q = (x @ Wq + bq).reshape(n, HEADS, HEAD_DIM)
        k = (x @ Wk + bk).reshape(n, HEADS, HEAD_DIM)
        v = (x @ Wv + bv).reshape(n, HEADS, HEAD_DIM)
        scores = jnp.einsum('ehd,ehd->eh', q[origin], k[dest]) * scale
        scores = scores * edge_weights
        seg_max = jax.ops.segment_max(scores, origin, num_segments=n)
        seg_max = jnp.where(jnp.isfinite(seg_max), seg_max, 0.0)
        e = jnp.exp(scores - seg_max[origin])
        denom = jax.ops.segment_sum(e, origin, num_segments=n)
        attn = e / (denom[origin] + 1e-16)
        weighted = attn[..., None] * v[dest]
        vals = jax.ops.segment_sum(weighted, origin, num_segments=n).reshape(n, DIM)
        out = vals @ Wo + bo
        mu = out.mean(-1, keepdims=True)
        var = ((out - mu) ** 2).mean(-1, keepdims=True)
        ln = (out - mu) * jax.lax.rsqrt(var + 1e-05) * gamma + beta
        return x + ln

    def _L2_gnn_ref(x, edge_index, Wl, Wr, att, bias):
        import jax, jax.numpy as jnp
        import numpy as np
        N = 6250
        E = 100000
        IN_C = 128
        HID = 16
        HEADS = 8
        NEG_SLOPE = 0.2

        def _gatv2_layer(x, src, dst, Wl, Wr, att, bias):
            n = x.shape[0]
            xl = (x @ Wl).reshape(n, HEADS, HID)
            xr = (x @ Wr).reshape(n, HEADS, HID)
            e = jax.nn.leaky_relu(xl[src] + xr[dst], NEG_SLOPE)
            score = jnp.einsum('ehc,hc->eh', e, att)
            m = jax.ops.segment_max(score, dst, num_segments=n)
            alpha = jnp.exp(score - m[dst])
            denom = jax.ops.segment_sum(alpha, dst, num_segments=n)
            alpha = alpha / denom[dst]
            out = jax.ops.segment_sum(alpha[:, :, None] * xl[src], dst, num_segments=n)
            return out.reshape(n, HEADS * HID) + bias
        n = x.shape[0]
        loops = jnp.arange(n, dtype=edge_index.dtype)
        src = jnp.concatenate([edge_index[0], loops])
        dst = jnp.concatenate([edge_index[1], loops])
        out = _gatv2_layer(x, src, dst, Wl, Wr, att, bias)
        return jax.nn.elu(out)

    def _L3_gnn_ref(x, edge_index, edge_weight, edge_attr, W_f1, b_f1, W_f2, b_f2, W_in, W_out, b_out, W_lin, b_lin):
        import jax, jax.numpy as jnp
        import numpy as np
        N_NODES = 5000
        N_EDGES = 80000
        HIDDEN = 128
        NUM_RBF = 50
        CUTOFF = 10.0
        src = edge_index[0]
        dst = edge_index[1]
        n_nodes = x.shape[0]
        C = 0.5 * (jnp.cos(edge_weight * (jnp.pi / CUTOFF)) + 1.0)
        Wf = jnp.tanh(edge_attr @ W_f1 + b_f1) @ W_f2 + b_f2
        Wf = Wf * C[:, None]
        h = x @ W_in
        msg = h[src] * Wf
        agg = jax.ops.segment_sum(msg, dst, num_segments=n_nodes)
        out = agg @ W_out + b_out
        out = jnp.tanh(out)
        return out @ W_lin + b_lin
    edge_index = jnp.stack([src, dst])
    x = _layernorm(x + _L0_gnn_ref(x, edge_index, L0_gnn_W, L0_gnn_src_attn, L0_gnn_dst_attn), axis=-1)
    x = _layernorm(x + _L1_gnn_ref(x, edge_index, edge_attr_8, L1_gnn_Wq, L1_gnn_bq, L1_gnn_Wk, L1_gnn_bk, L1_gnn_Wv, L1_gnn_bv, L1_gnn_Wo, L1_gnn_bo, L1_gnn_gamma, L1_gnn_beta), axis=-1)
    x = _layernorm(x + _L2_gnn_ref(x, edge_index, L2_gnn_Wl, L2_gnn_Wr, L2_gnn_att, L2_gnn_bias), axis=-1)
    x = _layernorm(x + _L3_gnn_ref(x, edge_index, edge_weight, edge_attr_50, L3_gnn_W_f1, L3_gnn_b_f1, L3_gnn_W_f2, L3_gnn_b_f2, L3_gnn_W_in, L3_gnn_W_out, L3_gnn_b_out, L3_gnn_W_lin, L3_gnn_b_lin), axis=-1)
    return x

_drawn_inputs = setup_inputs


def setup_inputs(seed=0):
    import zlib

    import numpy as np

    out = dict(_drawn_inputs(seed))
    spreads = {'L1_gnn_bq': (0.0, 0.317),
     'L1_gnn_bk': (0.0, 0.74),
     'L1_gnn_bv': (0.0, 0.1),
     'L1_gnn_bo': (0.0, 0.1),
     'L1_gnn_gamma': (1.0, 0.2),
     'L1_gnn_beta': (0.0, 0.1),
     'L3_gnn_b_f1': (0.0, 0.1),
     'L3_gnn_b_f2': (0.0, 0.1),
     'L3_gnn_b_out': (0.0, 0.1),
     'L3_gnn_b_lin': (0.0, 0.1)}
    factors = {'L2_gnn_bias': 5.443}
    for name, (base, spread) in spreads.items():
        noise = np.random.default_rng([zlib.crc32(name.encode()), seed]).standard_normal(out[name].shape)
        drawn = base * np.exp(spread * noise) if base else spread * noise
        out[name] = jnp.asarray(drawn.astype(out[name].dtype))
    for name, factor in factors.items():
        out[name] = (out[name] * factor).astype(out[name].dtype)
    return out
```

```python
from contextlib import ExitStack

import numpy as np

import concourse.bass as bass
from concourse import mybir

F32 = mybir.dt.float32
BF16 = mybir.dt.bfloat16
I32 = mybir.dt.int32
ALU = mybir.AluOpType
ACT = mybir.ActivationFunctionType
AX_X = mybir.AxisListType.X

P = 128
D = 128
H = 8
HD = D // H
CHUNKS = 16
STEP = 4
SLOTS = CHUNKS // STEP
RW = D + 2 * H
LOW = -1.0e30
EPS = 1e-5
SLOPE = 0.2
CUTOFF = 10.0
PI = float(np.pi)



def wide(ap, n):
    return ap.unsqueeze(len(ap.shape)).to_broadcast([*ap.shape, n])


def across(ap, n):
    return ap.unsqueeze(1).to_broadcast([ap.shape[0], n, *ap.shape[1:]])


class Chain:

    def __init__(self, eng, sem):
        self.eng, self.sem, self.start, self.n = eng, sem, 0, 0

    def link(self, ins):
        ins.then_inc(self.sem, 1)
        self.n += 1
        self.eng.wait_ge(self.sem, self.start + self.n)

    def turn(self, g):
        if isinstance(g, int) and g == 0:
            self.outer, self.n, self.per = self.start + self.n, 0, None
            self.start = self.outer
        else:
            self.per = self.per or self.n
            self.start, self.n = g * self.per + self.outer, 0

    def leave(self, turns):
        self.start, self.n = self.outer + turns * (self.per or self.n), 0


def turns(eng, count, body):
    body(0, True)
    if count > 1:
        with eng.Fori(1, count) as g:
            body(g, False)


class Machine:

    def __init__(self, nc, args, N, G, NB):
        self.nc, self.args, self.G, self.NB = nc, args, G, NB
        self.T = CHUNKS * G
        self.F = G * P
        self.N = N
        self.NT = -(-(-(-(N + 1) // P)) // NB) * NB
        self.NP = self.NT * P
        self.NI = self.NT // NB

        def dram(name, shape, dt=F32):
            return nc.dram_tensor(name, shape, dt).ap()
        T, NP = self.T, self.NP
        self.rec_by_src = dram("rec_by_src", (P * T, SREC), I32)
        self.sums = {n: dram(f"sums{n}", (T * P, n)) for n in (2 * H, D, RW)}
        self.spill = dram("spill", (G * SLOTS * P, STEP * D))
        self.x_now = dram("x_now", (NP, D))
        self.t_ssrc = dram("t_ssrc", (NP, H))
        self.t_sdst = dram("t_sdst", (NP, H))
        self.t_gat = dram("t_gat", (NP, D + 3 * H))
        self.t_q = dram("t_q", (NP, D))
        self.t_kv = dram("t_kv", (NP, 2 * D))
        self.t_xl = dram("t_xl", (NP, D))
        self.t_xr = dram("t_xr", (NP, D))
        self.t_h3 = dram("t_h3", (NP, D))
        self.chunk_ends = dram("chunk_ends", (P, 2))
        self.chunk_carry = dram("chunk_carry", (P + H, 1))

        sb = nc.alloc_sbuf_tensor
        self.ps = nc.alloc_psum_tensor("ps", [P, 8, 512], F32)
        self.ident = sb("ident", [P, P], F32)
        self.ident16 = sb("ident16", [P, P], BF16)
        self.lane = sb("lane", [P, 1], F32)
        self.column = sb("column", [P, P], F32)
        self.only_last = sb("only_last", [P, 2], F32)
        self.last_rank = sb("last_rank", [P, 2, self.NT], F32)
        self.first_rank = sb("first_rank", [P, 2, self.NT], F32)
        self.last_index = sb("last_index", [P, 2, self.NT], I32)

    def by_dst(self):
        return self.args["rec_by_dst"], 2, 1, 0

    def by_src(self):
        return self.rec_by_src.rearrange("(p t) c -> p (t c)", p=P), SREC, 0, 1


SREC = H + 2
BY_SRC, BY_DST = 0, 1


class stage:

    def __init__(self, m, name):
        self.m, self.name, self.k = m, name, 0

    def __enter__(self):
        self.guard = self.m.nc.cleanup_on_exit()
        self.guard.__enter__()
        return self

    def __exit__(self, *a):
        self.guard.__exit__(*a)
        self.m.nc.all_engine_barrier()

    def sem(self, name):
        return self.m.nc.alloc_semaphore(f"{self.name}_{name}")

    def sems(self, name, n=SLOTS):
        return [self.sem(f"{name}{b}") for b in range(n)]

    def sb(self, name, shape, dt=F32):
        return self.m.nc.alloc_sbuf_tensor(f"{self.name}_{name}", shape, dt)


def hold(eng, sem, n, spare):
    eng.wait_ge(sem, n)
    eng.sem_inc(spare, 1)


def constants(m):
    nc = m.nc
    with stage(m, "const") as s:
        counted, chain = s.sem("counted"), s.sem("chain")
        with nc.Block() as block:
            @block.gpsimd
            def _(pool):
                pool.iota(m.lane[:], [[0, 1]], base=0, channel_multiplier=1,
                          allow_small_or_imprecise_dtypes=True).then_inc(counted, 1)
                pool.iota(m.column[:], [[1, P]], base=0, channel_multiplier=0,
                          allow_small_or_imprecise_dtypes=True).then_inc(counted, 1)

            @block.vector
            def _(dve):
                ch = Chain(dve, chain)
                dve.wait_ge(counted, 2)
                ch.link(dve.tensor_scalar(m.ident[:], m.column[:], m.lane[:, 0:1], None, ALU.is_equal))
                ch.link(dve.tensor_scalar(m.ident16[:], m.column[:], m.lane[:, 0:1], None, ALU.is_equal))
                ch.link(dve.tensor_scalar(m.only_last[:, 0:1], m.lane[:], float(P - 1), None, ALU.is_equal))
                ch.link(dve.tensor_scalar(m.only_last[:, 1:2], m.only_last[:, 0:1], 1.0, None, ALU.subtract))



def count_edges(m, which, first_ranks):
    nc, T, NT, ps = m.nc, m.T, m.NT, m.ps
    U = 8
    field = 0 if which == BY_SRC else 1
    with stage(m, f"count{which}") as s:
        rec = s.sb("rec", [P, T, 2], I32)
        hi_i = s.sb("hi_i", [P, T], I32)
        idf, hi, lo = (s.sb(n, [P, T]) for n in ("idf", "hi", "lo"))
        hot_hi = s.sb("hot_hi", [P, 2, U, NT], BF16)
        hot_lo = s.sb("hot_lo", [P, 2, U, P], BF16)
        zero = s.sb("zero", [P, P], BF16)
        one = s.sb("one", [P, P])
        hist, last, before = (s.sb(n, [P, P]) for n in ("hist", "last", "before"))
        total, ahead = s.sb("total", [P, 1]), s.sb("ahead", [P, 1])
        rec_in, chain = s.sem("rec_in"), s.sem("chain")
        hots_ready, hots_used = s.sem("hots_ready"), s.sem("hots_used")
        zero_ready, hist_ready, total_ready = s.sem("zero_ready"), s.sem("hist_ready"), s.sem("total_ready")
        ahead_ready, ranks_ready, ranks_turned = s.sem("ahead_ready"), s.sem("ranks_ready"), s.sem("ranks_turned")
        assert T % (2 * U) == 0
        turns = T // (2 * U)
        with nc.Block() as block:
            @block.sync
            def _(sp):
                sp.dma_start(rec[:].rearrange("p t c -> p (t c)"), m.args["rec_by_dst"]).then_inc(rec_in, 16)

            @block.vector
            def _(dve):
                ch = Chain(dve, chain)
                ch.link(dve.memset(one[:], 1.0))
                dve.memset(zero[:], 0.0).then_inc(zero_ready, 1)
                dve.wait_ge(rec_in, 16)
                ch.link(dve.tensor_copy(idf[:], rec[:, :, field]))
                ch.link(dve.tensor_scalar(hi_i[:], rec[:, :, field], 7, None, ALU.logical_shift_right))
                ch.link(dve.tensor_copy(hi[:], hi_i[:]))
                ch.link(dve.scalar_tensor_tensor(lo[:], hi[:], float(-P), idf[:], ALU.mult, ALU.add))
                dve.sem_inc(hots_used, 2)
                with dve.Fori(0, turns) as c:
                    for k in range(2):
                        dve.wait_ge(hots_used, c * 2 + k + 1)
                        at = bass.ds(c * (2 * U) + k * U, U)
                        dve.tensor_tensor(hot_hi[:, k], across(m.column[:, 0:NT], U), wide(hi[:, at], NT),
                                          ALU.is_equal)
                        dve.tensor_tensor(hot_lo[:, k], across(m.column[:], U), wide(lo[:, at], P),
                                          ALU.is_equal).then_inc(hots_ready, 1)
                dve.wait_ge(hist_ready, 1)
                ch.link(dve.tensor_copy(hist[0:NT, :], ps[0:NT, 0, 0:P]))
                ch.link(dve.tensor_tensor_scan(last[0:NT, :], one[0:NT, :], hist[0:NT, :], 0.0,
                                               ALU.mult, ALU.add))
                ch.link(dve.tensor_copy(total[0:NT, :], last[0:NT, P - 1:P]))
                dve.tensor_scalar(before[0:NT, :], m.column[0:NT, :], m.lane[0:NT, 0:1], None,
                                  ALU.is_gt).then_inc(total_ready, 1)
                dve.wait_ge(ahead_ready, 1)
                ch.link(dve.tensor_copy(ahead[0:NT, :], ps[0:NT, 1, 0:1]))
                ch.link(dve.tensor_scalar(last[0:NT, :], last[0:NT, :], ahead[0:NT, 0:1], None, ALU.add))
                ch.link(dve.tensor_tensor(first_ranks[0:NT, :], last[0:NT, :], hist[0:NT, :], ALU.subtract))
                dve.tensor_scalar(last[0:NT, :], last[0:NT, :], -1.0, None, ALU.add).then_inc(ranks_ready, 1)
                dve.wait_ge(ranks_turned, 1)
                ch.link(dve.tensor_copy(m.last_rank[:, which, :], ps[:, 2, 0:NT]))
                ch.link(dve.tensor_copy(m.first_rank[:, which, :], ps[:, 3, 0:NT]))
                ch.link(dve.tensor_copy(m.last_index[:, which, :], m.last_rank[:, which, :]))

            @block.tensor
            def _(pe):
                pe.wait_ge(zero_ready, 1)
                pe.matmul(ps[0:NT, 0, 0:P], zero[:, 0:NT], zero[:], start=True, stop=False)
                with pe.Fori(0, turns) as c:
                    for k in range(2):
                        pe.wait_ge(hots_ready, c * 2 + k + 1)
                        for u in range(U):
                            ins = pe.matmul(ps[0:NT, 0, 0:P], hot_hi[:, k, u, :], hot_lo[:, k, u, :],
                                            start=False, stop=False)
                        ins.then_inc(hots_used, 1)
                pe.matmul(ps[0:NT, 0, 0:P], zero[:, 0:NT], zero[:], start=False, stop=True,
                          ).then_inc(hist_ready, 1)
                pe.wait_ge(total_ready, 1)
                pe.matmul(ps[0:NT, 1, 0:1], before[0:NT, 0:NT], total[0:NT, :], start=True,
                          stop=True).then_inc(ahead_ready, 1)
                pe.wait_ge(ranks_ready, 1)
                pe.transpose(ps[:, 2, 0:NT], last[0:NT, :], m.ident[0:NT, 0:NT])
                pe.transpose(ps[:, 3, 0:NT], first_ranks[0:NT, :], m.ident[0:NT, 0:NT]).then_inc(ranks_turned, 1)


def sort_by_src(m, next_rank):
    nc, T, G, NT, ps = m.nc, m.T, m.G, m.NT, m.ps
    with stage(m, "sort") as s:
        rec = s.sb("rec", [P, T, 2], I32)
        hi_i = s.sb("hi_i", [P, T], I32)
        idf, hi, lo = (s.sb(n, [P, T]) for n in ("idf", "hi", "lo"))
        hi_now = s.sb("hi_now", [P, 2, STEP], BF16)
        id_now = s.sb("id_now", [P, 2, STEP])
        earlier = s.sb("earlier", [P, P])
        chunk_tile = s.sb("chunk_tile", [P, CHUNKS])
        weight = s.sb("weight", [P, SLOTS, STEP * H])
        hot_hi = s.sb("hot_hi", [P, 2, STEP, NT], BF16)
        hot_lo = s.sb("hot_lo", [P, 2, STEP, P], BF16)
        hiT = s.sb("hiT", [P, STEP * P])
        same = s.sb("same", [P, STEP * P])
        part = s.sb("part", [P, 3, STEP])
        rank = s.sb("rank", [P, STEP])
        rank_i, tile_i = s.sb("rank_i", [P, STEP], I32), s.sb("tile_i", [P, STEP], I32)
        tile_no, chunk, pos = (s.sb(n, [P, STEP]) for n in ("tile_no", "chunk", "pos"))
        past = s.sb("past", [P, STEP, CHUNKS])
        pos_i = s.sb("pos_i", [P, SLOTS, STEP], I32)
        rec_out = s.sb("rec_out", [P, SLOTS, STEP, SREC], I32)
        rec_in, chain, spare = s.sem("rec_in"), s.sem("chain"), s.sem("spare")
        weight_in, sent = s.sems("weight_in"), s.sems("sent")
        (ids_ready, hots_ready, rows_ready, hiT_ready, looked_up, counted, next_ready, pos_ready,
         weights_ready) = (s.sem(n) for n in (
             "ids_ready", "hots_ready", "rows_ready", "hiT_ready", "looked_up", "counted", "next_ready",
             "pos_ready", "weights_ready"))
        with nc.Block() as block:
            @block.sync
            def _(sp):
                sp.dma_start(rec[:].rearrange("p t c -> p (t c)"), m.args["rec_by_dst"]).then_inc(rec_in, 16)

                def turn(g, first):
                    for b in range(SLOTS):
                        if not first:
                            sp.wait_ge(weights_ready, (g - 1) * SLOTS + b + 1)
                        sp.dma_start(weight[:, b],
                                     m.args["edge_attr_8"][:, bass.ds((g * SLOTS + b) * (STEP * H), STEP * H)]
                                     ).then_inc(weight_in[b], 16)
                turns(sp, G, turn)

            @block.gpsimd
            def _(pool):
                def turn(g, first):
                    for b in range(SLOTS):
                        hold(pool, weights_ready, g * SLOTS + b + 1, spare)
                        hold(pool, pos_ready, g * SLOTS + b + 1, spare)
                        for t in range(STEP):
                            pool.indirect_dma_start(
                                out=m.rec_by_src,
                                out_offset=bass.IndirectOffsetOnAxis(ap=pos_i[:, b, t:t + 1], axis=0),
                                in_=rec_out[:, b, t, :], in_offset=None).then_inc(sent[b], 16)
                turns(pool, G, turn)
                for b in range(SLOTS):
                    pool.wait_ge(sent[b], 16 * STEP * G)

            @block.scalar
            def _(act):
                def turn(g, first):
                    for b in range(SLOTS):
                        act.wait_ge(weight_in[b], (g + 1) * 16)
                        if not first:
                            act.wait_ge(sent[b], g * (16 * STEP))
                        act.activation(rec_out[:, b, :, 2:SREC].bitcast(F32),
                                       weight[:, b].rearrange("p (t c) -> p t c", c=H), ACT.Copy
                                       ).then_inc(weights_ready, 1)
                        act.wait_ge(counted, g * SLOTS + b + 1)
                        act.activation(next_rank[0:NT, :], ps[0:NT, 5, 0:P], ACT.Copy).then_inc(next_ready, 1)
                turns(act, G, turn)

            @block.tensor
            def _(pe):
                def turn(g, first):
                    for b in range(SLOTS):
                        k = g * SLOTS + b
                        if not (first and b == 0):
                            pe.wait_ge(pos_ready, k)
                        pe.wait_ge(ids_ready, k + 2)
                        for t in range(STEP):
                            pe.matmul(ps[0:NT, b % 2, t * P:(t + 1) * P],
                                      hi_now[:, b % 2, t:t + 1].to_broadcast([P, NT]),
                                      m.ident16[:], start=True, stop=True)
                            ins = pe.matmul(ps[:, 2 + b % 2, t * P:(t + 1) * P],
                                            id_now[:, b % 2, t:t + 1].to_broadcast([P, P]),
                                            m.ident[:], start=True, stop=True)
                        ins.then_inc(rows_ready, 1)
                        pe.wait_ge(hiT_ready, k + 1)
                        if not (first and b == 0):
                            pe.wait_ge(next_ready, k)
                        for t in range(STEP):
                            ins = pe.matmul(ps[:, 4, t * P:(t + 1) * P], hiT[0:NT, t * P:(t + 1) * P],
                                            next_rank[0:NT, :], start=True, stop=True)
                        ins.then_inc(looked_up, 1)
                        pe.matmul(ps[0:NT, 5, 0:P], m.ident[0:NT, 0:NT], next_rank[0:NT, :], start=True, stop=False)
                        for t in range(STEP):
                            ins = pe.matmul(ps[0:NT, 5, 0:P], hot_hi[:, b % 2, t, :], hot_lo[:, b % 2, t, :],
                                            start=False, stop=t == STEP - 1)
                        ins.then_inc(counted, 1)
                turns(pe, G, turn)

            @block.vector
            def _(dve):
                ch = Chain(dve, chain)
                dve.wait_ge(rec_in, 16)
                ch.link(dve.tensor_copy(idf[:], rec[:, :, 0]))
                ch.link(dve.tensor_scalar(hi_i[:], rec[:, :, 0], 7, None, ALU.logical_shift_right))
                ch.link(dve.tensor_copy(hi[:], hi_i[:]))
                ch.link(dve.scalar_tensor_tensor(lo[:], hi[:], float(-P), idf[:], ALU.mult, ALU.add))
                ch.link(dve.tensor_scalar(earlier[:], m.column[:], m.lane[:, 0:1], None, ALU.is_lt))
                ch.link(dve.memset(part[:], 0.0))
                ch.link(dve.tensor_scalar(chunk_tile[:], m.column[:, 0:CHUNKS], float(G), None, ALU.mult))
                dve.sem_inc(ids_ready, 1)

                def turn(g, first):
                    ch.turn(g)
                    for b in range(SLOTS):
                        k = g * SLOTS + b
                        at = bass.ds(k * STEP, STEP)
                        if not (first and b < 2):
                            dve.wait_ge(counted, k - 1)
                        ch.link(dve.tensor_copy(hi_now[:, b % 2, :], hi[:, at]))
                        ch.link(dve.tensor_copy(id_now[:, b % 2, :], idf[:, at]))
                        dve.sem_inc(ids_ready, 1)
                        dve.tensor_tensor(hot_hi[:, b % 2], across(m.column[:, 0:NT], STEP),
                                          wide(hi[:, at], NT), ALU.is_equal)
                        ch.link(dve.tensor_tensor(hot_lo[:, b % 2], across(m.column[:], STEP),
                                                  wide(lo[:, at], P), ALU.is_equal))
                        dve.wait_ge(rows_ready, k + 1)
                        dve.tensor_scalar(hiT[0:NT, :], ps[0:NT, b % 2, :], m.lane[0:NT, 0:1], None,
                                          ALU.is_equal).then_inc(hiT_ready, 1)
                        if not first:
                            dve.wait_ge(sent[b], g * (16 * STEP))
                        dve.tensor_copy(rec_out[:, b, :, 0:2], rec[:, at, :])
                        for t in range(STEP):
                            col = idf[:, bass.ds(k * STEP + t, 1)]
                            if t:
                                ch.link(dve.tensor_scalar(same[:, 0:t * P], ps[:, 2 + b % 2, 0:t * P], col, 0.0,
                                                          ALU.is_equal, ALU.add, accum_out=part[:, 1, t:t + 1]))
                            ch.link(dve.scalar_tensor_tensor(same[:, 0:P], ps[:, 2 + b % 2, t * P:(t + 1) * P],
                                                             col, earlier[:], ALU.is_equal, ALU.mult,
                                                             accum_out=part[:, 0, t:t + 1]))
                        dve.wait_ge(looked_up, k + 1)
                        for t in range(STEP):
                            ch.link(dve.scalar_tensor_tensor(same[:, 0:P], ps[:, 4, t * P:(t + 1) * P], 1.0,
                                                             hot_lo[:, b % 2, t, :], ALU.mult, ALU.mult,
                                                             accum_out=part[:, 2, t:t + 1]))
                        ch.link(dve.tensor_tensor(rank[:], part[:, 0, :], part[:, 2, :], ALU.add))
                        ch.link(dve.tensor_tensor(rank[:], rank[:], part[:, 1, :], ALU.add))
                        ch.link(dve.tensor_copy(rank_i[:], rank[:]))
                        ch.link(dve.tensor_scalar(tile_i[:], rank_i[:], 7, None, ALU.logical_shift_right))
                        ch.link(dve.tensor_copy(tile_no[:], tile_i[:]))
                        dve.tensor_tensor(past[:], wide(tile_no[:], CHUNKS), across(chunk_tile[:], STEP),
                                          ALU.is_ge)
                        ch.link(dve.scalar_tensor_tensor(pos[:], tile_no[:], float(-P), rank[:],
                                                         ALU.mult, ALU.add))
                        ch.link(dve.tensor_reduce(chunk[:], past[:], AX_X, ALU.add))
                        ch.link(dve.tensor_scalar(pos[:], pos[:], float(T), float(CHUNKS * G - 1),
                                                  ALU.mult, ALU.add))
                        ch.link(dve.scalar_tensor_tensor(pos[:], tile_no[:], float(CHUNKS), pos[:],
                                                         ALU.mult, ALU.add))
                        dve.scalar_tensor_tensor(pos_i[:, b, :], chunk[:], float(1 - CHUNKS * G), pos[:],
                                                 ALU.mult, ALU.add).then_inc(pos_ready, 1)
                turns(dve, G, turn)
                ch.leave(G)



def edge_scores(m, order, tables, name, scores, maxima, score_of, spill_from=None, rows=()):
    nc, G, ps = m.nc, m.G, m.ps
    rec_dram, rw, seg, _ = order
    with stage(m, name) as s:
        rec = s.sb("rec", [P, SLOTS, STEP, rw], I32)
        slot = [s.sb(f"rows{n}", [P, SLOTS, STEP, t.shape[1]]) for n, (t, _) in enumerate(tables)]
        tmp = s.sb("tmp", [P, 2, STEP, D])
        got = s.sb("got", [P, CHUNKS, H])
        ids = s.sb("ids", [P, CHUNKS, H])
        row_sb = [s.sb(f"row{n}", [P, r.shape[0]]) for n, r in enumerate(rows)]
        rec_in, gathered, spilled = s.sems("rec_in"), s.sems("gathered"), s.sems("spilled")
        rows_in, chain, spare = s.sem("rows_in"), s.sem("chain"), s.sem("spare")
        step_done, group_ready, turned, kept = (s.sem(n) for n in ("step_done", "group_ready", "turned", "kept"))
        per_step = 16 * STEP * len(tables)
        with nc.Block() as block:
            @block.sync
            def _(sp):
                for sb_row, r in zip(row_sb, rows):
                    sp.dma_start(sb_row[:], r.unsqueeze(0).to_broadcast([P, r.shape[0]])).then_inc(rows_in, 16)

                def turn(g, first):
                    for b in range(SLOTS):
                        if not first:
                            sp.wait_ge(step_done, (g - 1) * SLOTS + b + 1)
                        sp.dma_start(rec[:, b].rearrange("p t c -> p (t c)"),
                                     rec_dram[:, bass.ds((g * SLOTS + b) * (STEP * rw), STEP * rw)]
                                     ).then_inc(rec_in[b], 16)
                turns(sp, G, turn)

            @block.gpsimd
            def _(pool):
                def turn(g, first):
                    for b in range(SLOTS):
                        hold(pool, rec_in[b], (g + 1) * 16, spare)
                        if spill_from is not None and not first:
                            hold(pool, spilled[b], g * 16, spare)
                        for n, (table, field) in enumerate(tables):
                            for t in range(STEP):
                                pool.indirect_dma_start(
                                    out=slot[n][:, b, t, :], out_offset=None, in_=table,
                                    in_offset=bass.IndirectOffsetOnAxis(ap=rec[:, b, t, field:field + 1], axis=0),
                                ).then_inc(gathered[b], 16)
                turns(pool, G, turn)

            @block.scalar
            def _(act):
                def turn(g, first):
                    for b in range(SLOTS):
                        if spill_from is not None:
                            act.wait_ge(gathered[b], (g + 1) * per_step)
                            act.dma_start(
                                m.spill[bass.ds((g * SLOTS + b) * P, P), :].rearrange("p (t c) -> p t c", t=STEP),
                                slot[0][:, b, :, spill_from:spill_from + D]).then_inc(spilled[b], 16)
                    hold(act, turned, g + 1, spare)
                    at = bass.ds(g * P, P)
                    act.activation(scores[:, at], ps[:, 0, 0:P], ACT.Copy)
                    act.activation(maxima[:, at], ps[:, 0, P:2 * P], ACT.Copy).then_inc(kept, 1)
                turns(act, G, turn)
                if spill_from is not None:
                    for b in range(SLOTS):
                        act.wait_ge(spilled[b], 16 * G)

            @block.tensor
            def _(pe):
                def turn(g, first):
                    if not first:
                        pe.wait_ge(kept, g)
                    pe.wait_ge(group_ready, g + 1)
                    pe.transpose(ps[:, 0, 0:P], got[:].rearrange("p j h -> p (j h)"), m.ident[:])
                    pe.transpose(ps[:, 0, P:2 * P], ids[:].rearrange("p j h -> p (j h)"),
                                 m.ident[:]).then_inc(turned, 1)
                turns(pe, G, turn)

            @block.vector
            def _(dve):
                ch = Chain(dve, chain)
                if rows:
                    dve.wait_ge(rows_in, 16 * len(rows))

                def turn(g, first):
                    ch.turn(g)
                    for b in range(SLOTS):
                        dve.wait_ge(gathered[b], (g + 1) * per_step)
                        if b == 0 and not first:
                            dve.wait_ge(turned, g)
                        ch.link(dve.tensor_copy(ids[:, b * STEP:(b + 1) * STEP, :],
                                                wide(rec[:, b, :, seg], H)))
                        score_of(dve, ch, row_sb, [x[:, b] for x in slot], rec[:, b], tmp,
                                 got[:, b * STEP:(b + 1) * STEP, :])
                        dve.sem_inc(step_done, 1)
                    dve.sem_inc(group_ready, 1)
                turns(dve, G, turn)
                ch.leave(G)


def run_maxima(m, name, scores, maxima):
    nc, F, ps = m.nc, m.F, m.ps
    with stage(m, name) as s:
        starts = s.sb("starts", [P, F + 1], BF16)
        bound = s.sb("bound", [P, 2])
        ends = s.sb("ends", [P, 2])
        carried = s.sb("carried", [P, 1])
        line = s.sb("line", [H, CHUNKS, 2])
        linked = s.sb("linked", [H, CHUNKS])
        low = s.sb("low", [H, 1])
        moved, chain, give, diff = s.sem("moved"), s.sem("chain"), s.sem("give"), s.sem("diff")
        PIECES = 4
        cuts = [F * i // PIECES for i in range(PIECES + 1)]
        with nc.Block() as block:
            @block.sync
            def _(sp):
                sp.wait_ge(give, 1)
                sp.dma_start(bound[H:P, 0:1], maxima[0:P - H, F - 1:F]).then_inc(moved, 16)
                sp.dma_start(bound[0:P - H, 1:2], maxima[H:P, 0:1]).then_inc(moved, 16)
                sp.wait_ge(moved, 32)
                for way in range(2):
                    sp.wait_ge(give, 2 + 2 * way)
                    sp.dma_start(m.chunk_ends, ends[:]).then_inc(moved, 16)
                    sp.wait_ge(moved, 32 + way * 80 + 16)
                    sp.dma_start(line[:], m.chunk_ends.rearrange("(j h) c -> h j c", h=H)).then_inc(moved, 16)
                    sp.wait_ge(moved, 32 + way * 80 + 32)
                    sp.wait_ge(give, 3 + 2 * way)
                    carry = m.chunk_carry.rearrange("(j h) c -> h j c", h=H)
                    if way == 0:
                        sp.dma_start(carry[:, 1:CHUNKS + 1, :], linked[:].unsqueeze(2), allow_slow_non_contiguous=True).then_inc(moved, 16)
                        sp.dma_start(carry[:, 0:1, :], low[:].unsqueeze(2), allow_slow_non_contiguous=True).then_inc(moved, 16)
                    else:
                        sp.dma_start(carry[:, 0:CHUNKS, :], linked[:].unsqueeze(2), allow_slow_non_contiguous=True).then_inc(moved, 16)
                        sp.dma_start(carry[:, CHUNKS:CHUNKS + 1, :], low[:].unsqueeze(2), allow_slow_non_contiguous=True).then_inc(moved, 16)
                    sp.wait_ge(moved, 32 + way * 80 + 64)
                    first = 0 if way == 0 else H
                    sp.dma_start(carried[:], m.chunk_carry[first:first + P, :]).then_inc(moved, 16)
                    sp.wait_ge(moved, 32 + way * 80 + 80)

            @block.vector
            def _(dve):
                ch = Chain(dve, chain)
                ch.link(dve.memset(low[:], LOW))
                dve.memset(bound[:], -1.0).then_inc(give, 1)
                dve.wait_ge(moved, 32)
                dve.tensor_tensor(starts[:, 1:F], maxima[:, 1:F], maxima[:, 0:F - 1], ALU.not_equal)
                dve.tensor_tensor(starts[:, 0:1], maxima[:, 0:1], bound[:, 0:1], ALU.not_equal)
                ch.link(dve.tensor_tensor(starts[:, F:F + 1], maxima[:, F - 1:F], bound[:, 1:2], ALU.not_equal))
                ch.link(dve.tensor_scalar(starts[:], starts[:], LOW, None, ALU.mult))
                back = maxima[:, ::-1]
                for way in range(2):
                    flags = starts[:, 0:F] if way == 0 else starts[:, 1:F + 1]
                    end = F - 1 if way == 0 else 0

                    def scan(initial):
                        if way == 0:
                            return dve.tensor_tensor_scan(maxima[:], flags, scores[:], initial, ALU.add, ALU.max)
                        return dve.tensor_tensor_scan(back, starts[:, F:0:-1], back, initial, ALU.add, ALU.max)
                    ch.link(scan(LOW))
                    ch.link(dve.tensor_copy(ends[:, 0:1], maxima[:, end:end + 1]))
                    dve.tensor_reduce(ends[:, 1:2], flags, AX_X, ALU.min).then_inc(give, 1)
                    dve.wait_ge(moved, 32 + way * 80 + 32)
                    if way == 0:
                        dve.tensor_tensor_scan(linked[:], line[:, :, 1], line[:, :, 0], LOW,
                                               ALU.add, ALU.max).then_inc(give, 1)
                    else:
                        dve.tensor_tensor_scan(linked[:, ::-1], line[:, ::-1, 1], line[:, ::-1, 0], LOW,
                                               ALU.add, ALU.max).then_inc(give, 1)
                    dve.wait_ge(moved, 32 + way * 80 + 80)
                    ch.link(scan(carried[:, 0:1]))
                for a, z in zip(cuts, cuts[1:]):
                    dve.tensor_tensor(scores[:, a:z], scores[:, a:z], maxima[:, a:z], ALU.subtract
                                      ).then_inc(diff, 1)

            @block.scalar
            def _(act):
                for n, (a, z) in enumerate(zip(cuts, cuts[1:])):
                    act.wait_ge(diff, n + 1)
                    act.activation(scores[:, a:z], scores[:, a:z], ACT.Exp)



STATS, GAT, SOFT, FILTER = "stats", "gat", "soft", "filter"


def sum_runs(m, order, name, kind, scores=None, maxima=None):
    nc, G, T, ps, args = m.nc, m.G, m.T, m.ps, m.args
    rec_dram, rw, seg, other = order
    msg_cols = {STATS: slice(D, D + H), GAT: slice(0, D), SOFT: slice(0, D + H), FILTER: slice(0, D)}[kind]
    out_cols = {STATS: slice(D, RW), GAT: slice(0, D), SOFT: slice(0, RW), FILTER: slice(0, D)}[kind]
    width = msg_cols.stop - msg_cols.start
    tables = {STATS: [], GAT: [(m.t_gat, other), (m.t_ssrc, seg)], SOFT: [], FILTER: [(m.t_h3, other)]}[kind]
    weighted = kind in (STATS, SOFT)
    per_step = 16 * STEP * len(tables)
    with stage(m, name) as s:
        rec = s.sb("rec", [P, SLOTS, STEP, rw], I32)
        slot = [s.sb(f"rows{n}", [P, SLOTS, STEP, t.shape[1]]) for n, (t, _) in enumerate(tables)]
        if kind == SOFT:
            kept_rows = s.sb("kept_rows", [P, SLOTS, STEP, D])
        segs = s.sb("segs", [P, CHUNKS])
        carry_id = s.sb("carry_id", [P, SLOTS, STEP])
        same = s.sb("same", [P, 2, STEP, P])
        goes_on = s.sb("goes_on", [P, 2, STEP, P])
        msg = s.sb("msg", [P, 2, STEP, D + H])
        run = s.sb("run", [P, CHUNKS, RW])
        if weighted:
            by_run = s.sb("by_run", [P, 2, P])
            pm = s.sb("pm", [P, 2, CHUNKS, H])
        if kind == GAT:
            coef = s.sb("coef", [P, 2, STEP, H])
        if kind == FILTER:
            attr = s.sb("attr", [args["W_f1"].shape[0], SLOTS, STEP * P])
            w1, w2 = s.sb("w1", list(args["W_f1"].shape)), s.sb("w2", [D, D])
            b1, b2 = s.sb("b1", [D, 1]), s.sb("b2", [1, D])
            one_row = s.sb("one_row", [1, P])
            cut, whole = s.sb("cut", [P, T]), s.sb("whole", [P, T])
            hidden = s.sb("hidden", [D, STEP * P])
        rec_in, gathered, stored, kept_in, attr_in = (s.sems(n) for n in (
            "rec_in", "gathered", "stored", "kept_in", "attr_in"))
        apart = s.sem("apart")
        (chain, spare, step_done, segs_ready, rows_ready, sel_ready, msg_ready, summed, evacuated, turned,
         pm_ready, coef_ready, exp_ready, const_in, half_ready, cut_ready, hid_sum, hid_ready, filt_ready
         ) = (s.sem(n) for n in (
             "chain", "spare", "step_done", "segs_ready", "rows_ready", "sel_ready", "msg_ready", "summed",
             "evacuated", "turned", "pm_ready", "coef_ready", "exp_ready", "const_in", "half_ready", "cut_ready",
             "hid_sum", "hid_ready", "filt_ready"))

        def sums_of(b):
            first = 2 + 2 * (b % 2)
            return ps[:, first:first + 2, :].rearrange("p b (u c) -> p b u c", u=2)

        with nc.Block() as block:
            @block.sync
            def _(sp):
                if kind == FILTER:
                    sp.dma_start(w1[:], args["W_f1"]).then_inc(const_in, 16)
                    sp.dma_start(w2[:], args["W_f2"]).then_inc(const_in, 16)
                    sp.dma_start(b1[:], args["b_f1"].unsqueeze(1)).then_inc(const_in, 16)
                    sp.dma_start(b2[:], args["b_f2"].unsqueeze(0)).then_inc(const_in, 16)
                    sp.dma_start(cut[:], args["edge_weight"]).then_inc(const_in, 16)

                def turn(g, first):
                    for b in range(SLOTS):
                        if not first:
                            sp.wait_ge(step_done, (g - 1) * SLOTS + b + 1)
                        sp.dma_start(rec[:, b].rearrange("p t c -> p (t c)"),
                                     rec_dram[:, bass.ds((g * SLOTS + b) * (STEP * rw), STEP * rw)]
                                     ).then_inc(rec_in[b], 16)
                        if kind == SOFT:
                            sp.dma_start(kept_rows[:, b].rearrange("p t c -> p (t c)"),
                                         m.spill[bass.ds((g * SLOTS + b) * P, P), :]).then_inc(kept_in[b], 16)
                        if kind == FILTER:
                            sp.dma_start(attr[:, b, :],
                                         args["edge_attr_50"][:, bass.ds((g * SLOTS + b) * (STEP * P), STEP * P)]
                                         ).then_inc(attr_in[b], 16)
                turns(sp, G, turn)

            if tables:
                @block.gpsimd
                def _(pool):
                    def turn(g, first):
                        for b in range(SLOTS):
                            hold(pool, rec_in[b], (g + 1) * 16, spare)
                            for n, (table, field) in enumerate(tables):
                                for t in range(STEP):
                                    pool.indirect_dma_start(
                                        out=slot[n][:, b, t, :], out_offset=None, in_=table,
                                        in_offset=bass.IndirectOffsetOnAxis(ap=rec[:, b, t, field:field + 1],
                                                                            axis=0)).then_inc(gathered[b], 16)
                    turns(pool, G, turn)

            @block.tensor
            def _(pe):
                if kind == FILTER:
                    pe.wait_ge(const_in, 80)

                def turn(g, first):
                    if weighted:
                        pe.wait_ge(apart, g + 1)
                        pe.transpose(ps[:, 6, 0:P], by_run[:, 0, :], m.ident[:])
                        pe.transpose(ps[:, 6, P:2 * P], by_run[:, 1, :], m.ident[:]).then_inc(turned, 1)
                    for b in range(SLOTS):
                        k = g * SLOTS + b
                        if not (first and b < 2):
                            pe.wait_ge(sel_ready, k - 1)
                        pe.wait_ge(segs_ready, k + 1)
                        for t in range(STEP):
                            j = b * STEP + t
                            ins = pe.matmul(ps[:, b % 2, t * P:(t + 1) * P],
                                            segs[:, j:j + 1].to_broadcast([P, P]), m.ident[:],
                                            start=True, stop=True)
                        ins.then_inc(rows_ready, 1)
                        if kind == FILTER:
                            if not (first and b == 0):
                                pe.wait_ge(hid_ready, k)
                            pe.wait_ge(attr_in[b], (g + 1) * 16)
                            pe.matmul(ps[:, 6, :], w1[:], attr[:, b, :], start=True, stop=True
                                      ).then_inc(hid_sum, 1)
                            if not (first and b == 0):
                                pe.wait_ge(msg_ready, k)
                            pe.wait_ge(hid_ready, k + 1)
                            for t in range(STEP):
                                part = ps[:, 7, t * P:(t + 1) * P]
                                pe.matmul(part, hidden[:, t * P:(t + 1) * P], w2[:], start=True, stop=False)
                                ins = pe.matmul(part, one_row[:], b2[:], start=False, stop=True)
                            ins.then_inc(filt_ready, 1)
                        if not (first and b < 2):
                            pe.wait_ge(evacuated, k - 1)
                        pe.wait_ge(sel_ready, k + 1)
                        pe.wait_ge(msg_ready, k + 1)
                        for t in range(STEP):
                            part = sums_of(b)[:, t // 2, t % 2, 0:width]
                            pe.matmul(part, same[:, b % 2, t, :], msg[:, b % 2, t, msg_cols],
                                      start=True, stop=False)
                            ins = pe.matmul(part, goes_on[:, b % 2, t, :], run[:, b * STEP + t, msg_cols],
                                            start=False, stop=True)
                        ins.then_inc(summed, 1)
                turns(pe, G, turn)

            @block.scalar
            def _(act):
                if kind == FILTER:
                    act.wait_ge(const_in, 80)
                    act.wait_ge(half_ready, 1)
                    act.activation(cut[:], cut[:], ACT.Sin, scale=PI).then_inc(cut_ready, 1)

                def turn(g, first):
                    if weighted:
                        at = bass.ds(g * P, P)
                        act.activation(by_run[:, 0, :], scores[:, at], ACT.Copy)
                        act.activation(by_run[:, 1, :], maxima[:, at], ACT.Copy).then_inc(apart, 1)
                        act.wait_ge(turned, g + 1)
                        if not first:
                            act.wait_ge(msg_ready, g * SLOTS)
                        act.activation(pm[:].rearrange("p a j h -> p (a j h)"), ps[:, 6, 0:2 * P], ACT.Copy
                                       ).then_inc(pm_ready, 1)
                    for b in range(SLOTS):
                        k = g * SLOTS + b
                        if kind == GAT:
                            act.wait_ge(coef_ready, k + 1)
                            act.activation(coef[:, b % 2], coef[:, b % 2], ACT.Exp).then_inc(exp_ready, 1)
                        if kind == FILTER:
                            act.wait_ge(hid_sum, k + 1)
                            act.activation(hidden[:], ps[:, 6, :], ACT.Tanh, bias=b1[:, 0:1]).then_inc(hid_ready, 1)
                        act.wait_ge(summed, k + 1)
                        if not first:
                            act.wait_ge(stored[b], g * 16)
                        tiles = slice(b * STEP, (b + 1) * STEP)
                        act.activation(run[:, tiles, msg_cols].rearrange("p (b u) c -> p b u c", u=2),
                                       sums_of(b)[:, :, :, 0:width], ACT.Copy).then_inc(evacuated, 1)
                        act.wait_ge(msg_ready, k + 1)
                        act.wait_ge(evacuated, k + 1)
                        act.dma_start(
                            m.sums[out_cols.stop - out_cols.start].rearrange("(j g p) c -> p g j c", g=G, p=P)[
                                :, bass.ds(g, 1), tiles, :],
                            run[:, tiles, out_cols].unsqueeze(1)).then_inc(stored[b], 16)
                turns(act, G, turn)
                for b in range(SLOTS):
                    act.wait_ge(stored[b], 16 * G)

            @block.vector
            def _(dve):
                ch = Chain(dve, chain)
                ch.link(dve.memset(segs[:], -1.0))
                ch.link(dve.memset(run[:], 0.0))
                if kind == FILTER:
                    dve.memset(one_row[:], 1.0)
                    dve.wait_ge(const_in, 80)
                    ch.link(dve.tensor_scalar(cut[:], cut[:], 0.5 / CUTOFF, None, ALU.mult))
                    ch.link(dve.tensor_scalar(whole[:], cut[:], ROUND, None, ALU.add))
                    ch.link(dve.tensor_scalar(whole[:], whole[:], -ROUND, None, ALU.add))
                    dve.tensor_tensor(cut[:], cut[:], whole[:], ALU.subtract).then_inc(half_ready, 1)
                    dve.wait_ge(cut_ready, 1)
                    ch.link(dve.tensor_tensor(cut[:], cut[:], cut[:], ALU.mult))
                    ch.link(dve.tensor_scalar(cut[:], cut[:], -1.0, 1.0, ALU.mult, ALU.add))

                def turn(g, first):
                    ch.turn(g)
                    for b in range(SLOTS):
                        k = g * SLOTS + b
                        tiles = slice(b * STEP, (b + 1) * STEP)
                        dve.wait_ge(rec_in[b], (g + 1) * 16)
                        ch.link(dve.tensor_scalar(carry_id[:, b, :], segs[:, tiles], m.only_last[:, 0:1],
                                                  m.only_last[:, 1:2], ALU.mult, ALU.add))
                        ch.link(dve.tensor_copy(segs[:, tiles], rec[:, b, :, seg]))
                        dve.sem_inc(segs_ready, 1)
                        if not (first and b < 2):
                            dve.wait_ge(summed, k - 1)
                        out = msg[:, b % 2]
                        if tables:
                            dve.wait_ge(gathered[b], (g + 1) * per_step)
                        if kind == GAT:
                            rows, ssrc, c = slot[0][:, b], slot[1][:, b], coef[:, b % 2]
                            ch.link(dve.tensor_tensor(c, ssrc, rows[:, :, D:D + H], ALU.add))
                            ch.link(dve.scalar_tensor_tensor(c, c, SLOPE, c, ALU.mult, ALU.max))
                            ch.link(dve.tensor_tensor(c, c, rows[:, :, D + 2 * H:D + 3 * H], ALU.subtract))
                            dve.sem_inc(coef_ready, 1)
                            dve.wait_ge(exp_ready, k + 1)
                            ch.link(dve.tensor_tensor(c, c, rows[:, :, D + H:D + 2 * H], ALU.mult))
                            values, weights = rows[:, :, 0:D], c
                        if weighted:
                            dve.wait_ge(pm_ready, g + 1)
                            weights = pm[:, 0, tiles, :]
                            if not first:
                                dve.wait_ge(stored[b], g * 16)
                            dve.tensor_copy(run[:, tiles, D + H:RW], pm[:, 1, tiles, :])
                            ch.link(dve.tensor_copy(out[:, :, D:D + H], weights))
                        if kind == SOFT:
                            dve.wait_ge(kept_in[b], (g + 1) * 16)
                            values = kept_rows[:, b]
                        if kind in (GAT, SOFT):
                            for t in range(STEP):
                                last = dve.tensor_tensor(
                                    out[:, t, 0:D].rearrange("p (h c) -> p h c", h=H),
                                    values[:, t, :].rearrange("p (h c) -> p h c", h=H),
                                    wide(weights[:, t, :], HD), ALU.mult)
                            ch.link(last)
                        if kind == FILTER:
                            dve.wait_ge(filt_ready, k + 1)
                            for t in range(STEP):
                                last = dve.scalar_tensor_tensor(
                                    out[:, t, 0:D], ps[:, 7, t * P:(t + 1) * P],
                                    cut[:, bass.ds(k * STEP + t, 1)], slot[0][:, b, t, :], ALU.mult, ALU.mult)
                            ch.link(last)
                        dve.sem_inc(msg_ready, 1)
                        dve.wait_ge(rows_ready, k + 1)
                        id_rows = ps[:, b % 2, :].rearrange("p (t c) -> p t c", c=P)
                        dve.tensor_tensor(same[:, b % 2], id_rows, wide(segs[:, tiles], P), ALU.is_equal)
                        ch.link(dve.tensor_tensor(goes_on[:, b % 2], id_rows, wide(carry_id[:, b, :], P),
                                                  ALU.is_equal))
                        dve.sem_inc(sel_ready, 1)
                        dve.sem_inc(step_done, 1)
                turns(dve, G, turn)
                ch.leave(G)


ROUND = 1.5 * 2.0 ** 23



class BlockView:
    pass


def node_stage(m, name, steps, products, asks=(), fetch=None, cols=None, weights=(), rows=(), features=None,
               turned_in=None, buffers=(), stores=(), also=()):
    nc, NB, NI, F, ps = m.nc, m.NB, m.NI, m.F, m.ps
    with stage(m, name) as s:
        v = BlockView()
        v.m, v.s, v.ps, v.NB = m, s, ps, NB
        v.x = s.sb("x", [P, NB, D])
        v.y = s.sb("y", [P, NB, D])
        v.tmp = s.sb("tmp", [P, NB, D])
        v.yT = s.sb("yT", [P, NB * P])
        v.small = s.sb("small", [P, 2, NB])
        v.row = [s.sb(f"row{n}", [P, r.shape[0]]) for n, r in enumerate(rows)]
        v.w = [s.sb(f"w{n}", [P, w.shape[1]]) for n, w in enumerate(weights)]
        v.buf = {n: s.sb(n, [P, NB, width]) for n, width in buffers}
        v.buf["y"] = v.y
        const_in, chain, spare, x_in, stored, block_free, block_done = (s.sem(n) for n in (
            "const_in", "chain", "spare", "x_in", "stored", "block_free", "block_done"))
        given, made, asked, answered, idx_ready, fetched = (s.sem(n) for n in (
            "given", "made", "asked", "answered", "idx_ready", "fetched"))
        pe_steps = list(products)
        if fetch is not None:
            sums = m.sums[cols.stop - cols.start]
            v.sums = s.sb("sums", [P, NB, RW])
            idx = s.sb("idx", [P, NB], I32)
            cross, before = s.sb("cross", [P, NB, CHUNKS]), s.sb("before", [P, NB, CHUNKS])
            crossT = s.sb("crossT", [CHUNKS, NB * P])
            tails = s.sb("tails", [CHUNKS, RW])
            tail_rank = s.sb("tail_rank", [P, CHUNKS])
            v.mask = s.sb("mask", [P, NB])

            def turn_cross(pe):
                for t in range(NB):
                    ins = pe.transpose(ps[0:CHUNKS, t // 4, (t % 4) * P:(t % 4 + 1) * P], cross[:, t, :],
                                       m.ident[:])
                return ins

            def add_tails(pe):
                for t in range(NB):
                    ins = pe.matmul(ps[:, 2 + t // 3, (t % 3) * RW:(t % 3) * RW + cols.stop - cols.start],
                                    crossT[:, t * P:(t + 1) * P], tails[:, cols], start=True, stop=True)
                return ins
            pe_steps = [turn_cross, add_tails] + pe_steps
        n_const = 16 * (len(weights) + len(rows) + (fetch is not None))
        NPROD, NASK = len(pe_steps), len(asks)

        def block_rows(table, g, a, z):
            return table[bass.ds(g * (NB * P), NB * P), a:z].rearrange("(t p) c -> p t c", p=P)

        with nc.Block() as block:
            @block.sync
            def _(sp):
                for w, d in zip(v.w, weights):
                    sp.dma_start(w[:], d).then_inc(const_in, 16)
                for r, d in zip(v.row, rows):
                    sp.dma_start(r[:], d.unsqueeze(0).to_broadcast([P, d.shape[0]])).then_inc(const_in, 16)
                if fetch is not None:
                    sp.dma_start(tails[:, cols], sums.rearrange("(j f) c -> j f c", f=F)[:, F - 1, :]
                                 ).then_inc(const_in, 16)

                def turn(g, first):
                    if not first:
                        sp.wait_ge(block_done, g)
                    if turned_in is not None:
                        sp.dma_start(v.yT[:], turned_in[:, bass.ds(g * (NB * P), NB * P)]).then_inc(x_in, 16)
                    else:
                        sp.dma_start(v.x[:], block_rows(features if features is not None else m.x_now, g, 0, D)
                                     ).then_inc(x_in, 16)
                    for n, table in also:
                        sp.dma_start(v.buf[n][:], block_rows(table, g, 0, table.shape[1])).then_inc(x_in, 16)
                turns(sp, NI, turn)

            if fetch is not None:
                @block.gpsimd
                def _(pool):
                    def turn(g, first):
                        hold(pool, idx_ready, g + 1, spare)
                        for t in range(NB):
                            pool.indirect_dma_start(
                                out=v.sums[:, t, cols], out_offset=None, in_=sums,
                                in_offset=bass.IndirectOffsetOnAxis(ap=idx[:, t:t + 1], axis=0)
                            ).then_inc(fetched, 16)
                    turns(pool, NI, turn)

            @block.tensor
            def _(pe):
                pe.wait_ge(const_in, n_const)

                def turn(g, first):
                    for n, product in enumerate(pe_steps):
                        pe.wait_ge(given, g * NPROD + n + 1)
                        ins = product(pe) if (fetch is not None and n < 2) else product(v, pe)
                        ins.then_inc(made, 1)
                turns(pe, NI, turn)

            @block.scalar
            def _(act):
                def turn(g, first):
                    for n, ask in enumerate(asks):
                        act.wait_ge(asked, g * NASK + n + 1)
                        ask(v, act).then_inc(answered, 1)
                    act.wait_ge(block_done, g + 1)
                    for table, a, z, name_of in stores:
                        act.dma_start(block_rows(table, g, a, z), v.buf[name_of][:, :, 0:z - a]
                                      ).then_inc(stored, 16)
                turns(act, NI, turn)
                act.wait_ge(stored, 16 * len(stores) * NI)

            @block.vector
            def _(dve):
                ch = Chain(dve, chain)
                v.dve, v.link = dve, ch.link
                dve.wait_ge(const_in, n_const) if n_const else None
                if fetch is not None:
                    ch.link(dve.tensor_scalar(tail_rank[:], m.column[:, 0:CHUNKS], float(F), float(F - 1),
                                              ALU.mult, ALU.add))

                def turn(g, first):
                    ch.turn(g)
                    v.g, count = g, {"made": 0, "answered": 0}

                    def give():
                        dve.sem_inc(given, 1)

                    def made_wait():
                        count["made"] += 1
                        dve.wait_ge(made, g * NPROD + count["made"])

                    def ask():
                        dve.sem_inc(asked, 1)
                        count["answered"] += 1
                        dve.wait_ge(answered, g * NASK + count["answered"])

                    def results_free():
                        if not first:
                            dve.wait_ge(stored, g * (16 * len(stores)))
                    v.give, v.made, v.ask, v.results_free = give, made_wait, ask, results_free
                    if fetch is not None:
                        at = bass.ds(g * NB, NB)
                        lr, fr = m.last_rank[:, fetch, at], m.first_rank[:, fetch, at]
                        ch.link(dve.tensor_scalar(idx[:], m.last_index[:, fetch, at], 0.0, None, ALU.max))
                        dve.sem_inc(idx_ready, 1)
                        dve.tensor_tensor(v.mask[:], lr, fr, ALU.is_ge)
                        dve.tensor_tensor(cross[:], across(tail_rank[:], NB), wide(fr, CHUNKS), ALU.is_ge)
                        ch.link(dve.tensor_tensor(before[:], across(tail_rank[:], NB), wide(lr, CHUNKS),
                                                  ALU.is_lt))
                        ch.link(dve.tensor_tensor(cross[:], cross[:], before[:], ALU.mult))
                        give()
                        made_wait()
                        for a in range(0, NB, 4):
                            n = min(4, NB - a) * P
                            last = dve.tensor_copy(crossT[:, a * P:a * P + n], ps[0:CHUNKS, a // 4, 0:n])
                        ch.link(last)
                        give()
                        dve.wait_ge(fetched, (g + 1) * (16 * NB))
                        ch.link(dve.tensor_tensor(v.sums[:, :, cols], v.sums[:, :, cols],
                                                  wide(v.mask[:], cols.stop - cols.start), ALU.mult))
                        made_wait()
                        added = slice(cols.start, min(cols.stop, D + H))
                        for a in range(0, NB, 3):
                            n = min(3, NB - a)
                            part = ps[:, 2 + a // 3, 0:n * RW].rearrange("p (t c) -> p t c", c=RW)
                            last = dve.tensor_tensor(v.sums[:, a:a + n, added], v.sums[:, a:a + n, added],
                                                     part[:, :, 0:added.stop - added.start], ALU.add)
                        ch.link(last)
                    dve.wait_ge(x_in, (g + 1) * (16 * (1 + len(also))))
                    steps(v)
                    assert count["made"] == NPROD and count["answered"] == NASK, (count, NPROD, NASK)
                    dve.sem_inc(block_done, 1)
                turns(dve, NI, turn)
                ch.leave(NI)


def pieces(v, bank):
    return [(slice(a, min(a + 4, v.NB)),
             v.ps[:, bank + a // 4, 0:(min(a + 4, v.NB) - a) * P].rearrange("p (t c) -> p t c", c=P))
            for a in range(0, v.NB, 4)]


def turn_into(src, bank):
    def product(v, pe):
        for t in range(v.NB):
            ins = pe.transpose(v.ps[:, bank + t // 4, (t % 4) * P:(t % 4 + 1) * P],
                               v.buf[src][:, t, :], v.m.ident[:])
        return ins
    return product


def times(w, bank):
    def product(v, pe):
        for t in range(v.NB):
            ins = pe.matmul(v.ps[:, bank + t // 4, (t % 4) * P:(t % 4 + 1) * P], v.yT[:, t * P:(t + 1) * P],
                            v.w[w][:], start=True, stop=True)
        return ins
    return product


def turned(v):
    v.give()
    v.made()
    for tiles, part in pieces(v, 0):
        last = v.dve.tensor_copy(v.yT[:, tiles.start * P:tiles.stop * P], part.rearrange("p t c -> p (t c)"))
    v.link(last)


def add_row(v, out, bank, row):
    for tiles, part in pieces(v, bank):
        last = v.dve.tensor_tensor(out[:, tiles, :], part, across(row, tiles.stop - tiles.start), ALU.add)
    v.link(last)


def normalise(v, out, x):
    dve, link = v.dve, v.link
    mean, var = v.small[:, 0, :], v.small[:, 1, :]
    link(dve.tensor_reduce(mean, x, AX_X, ALU.add))
    link(dve.tensor_scalar(mean, mean, 1.0 / D, None, ALU.mult))
    link(dve.tensor_tensor(out, x, wide(mean, D), ALU.subtract))
    link(dve.tensor_tensor(v.tmp[:], out, out, ALU.mult))
    link(dve.tensor_reduce(var, v.tmp[:], AX_X, ALU.add))
    link(dve.tensor_scalar(var, var, 1.0 / D, EPS, ALU.mult, ALU.add))
    v.ask()
    link(dve.reciprocal(var, var))
    link(dve.tensor_tensor(out, out, wide(var, D), ALU.mult))


def root(v, act):
    return act.activation(v.small[:, 1, :], v.small[:, 1, :], ACT.Sqrt)


def by_head(ap):
    return ap.rearrange("p t (h c) -> p (t h) c", h=H)


def flat_heads(ap):
    return ap.rearrange("p t h -> p (t h)")



def build(nc, args, out, N, G, NB):
    m = Machine(nc, args, N, G, NB)
    constants(m)
    a = args

    def start(v):
        v.results_free()
        v.give()
        v.made()
        for tiles, part in pieces(v, 0):
            last = v.dve.tensor_copy(v.buf["h"][:, tiles, :], part)
        v.link(last)
        for row, dst in ((0, v.buf["ssrc"]), (1, v.buf["sdst"])):
            v.link(v.dve.tensor_tensor(v.tmp[:], v.buf["h"][:], across(v.row[row][:], v.NB), ALU.mult))
            v.link(v.dve.tensor_reduce(flat_heads(dst[:]), by_head(v.tmp[:]), AX_X, ALU.add))
    node_stage(m, "n0", start, [times(0, 0)], weights=[a["W"]], rows=[a["src_attn"], a["dst_attn"]],
               turned_in=a["xT"], buffers=[("h", D), ("ssrc", H), ("sdst", H)],
               stores=[(m.t_ssrc, 0, H, "ssrc"), (m.t_sdst, 0, H, "sdst"), (m.t_gat, 0, D, "h"),
                       (m.t_gat, D, D + H, "sdst")])

    next_rank = nc.alloc_sbuf_tensor("next_rank", [P, P], F32)
    count_edges(m, BY_DST, next_rank)
    count_edges(m, BY_SRC, next_rank)
    sort_by_src(m, next_rank)

    guard = nc.cleanup_on_exit()
    guard.__enter__()
    scores = nc.alloc_sbuf_tensor("scores", [P, m.F], F32)
    maxima = nc.alloc_sbuf_tensor("maxima", [P, m.F], F32)

    def gat_score(dve, ch, row, rows, rec, tmp, got):
        c = tmp[:, 0, :, 0:H]
        ch.link(dve.tensor_tensor(c, rows[0], rows[1], ALU.add))
        ch.link(dve.scalar_tensor_tensor(got, c, SLOPE, c, ALU.mult, ALU.max))
    edge_scores(m, m.by_dst(), [(m.t_ssrc, 0), (m.t_sdst, 1)], "e0", scores, maxima, gat_score)
    run_maxima(m, "m0", scores, maxima)
    sum_runs(m, m.by_dst(), "s0", STATS, scores, maxima)

    def stats(v):
        v.results_free()
        v.link(v.dve.tensor_scalar(v.buf["none"][:], v.mask[:].unsqueeze(2), -1.0, 1.0, ALU.mult, ALU.add))
        v.link(v.dve.tensor_tensor(v.buf["stat"][:, :, 0:H], v.sums[:, :, D:D + H], v.buf["none"][:].to_broadcast([P, v.NB, H]),
                                   ALU.add))
        v.link(v.dve.reciprocal(v.buf["stat"][:, :, 0:H], v.buf["stat"][:, :, 0:H]))
        v.link(v.dve.tensor_copy(v.buf["stat"][:, :, H:2 * H], v.sums[:, :, D + H:RW]))
    node_stage(m, "n1", stats, [], fetch=BY_DST, cols=slice(D, RW), features=a["x"],
               buffers=[("stat", 2 * H), ("none", 1)], stores=[(m.t_gat, D + H, D + 3 * H, "stat")])
    sum_runs(m, m.by_src(), "s1", GAT)

    def attention_in(v):
        v.results_free()
        v.link(v.dve.tensor_tensor(v.x[:], v.x[:], v.sums[:, :, 0:D], ALU.add))
        normalise(v, v.y[:], v.x[:])
        turned(v)
        v.give()
        v.give()
        v.give()
        v.made()
        add_row(v, v.buf["q"], 2, v.row[0][:])
        v.made()
        add_row(v, v.buf["kv"][:, :, 0:D], 4, v.row[1][:])
        v.made()
        add_row(v, v.buf["kv"][:, :, D:2 * D], 6, v.row[2][:])
    node_stage(m, "n2", attention_in, [turn_into("y", 0), times(0, 2), times(1, 4), times(2, 6)], [root],
               fetch=BY_SRC, cols=slice(0, D), features=a["x"], weights=[a["Wq"], a["Wk"], a["Wv"]],
               rows=[a["bq"], a["bk"], a["bv"]], buffers=[("q", D), ("kv", 2 * D)],
               stores=[(m.x_now, 0, D, "y"), (m.t_q, 0, D, "q"), (m.t_kv, 0, 2 * D, "kv")])

    def attention_score(dve, ch, row, rows, rec, tmp, got):
        kv, q = rows
        t = tmp[:, 0]
        ch.link(dve.tensor_tensor(t, q, kv[:, :, 0:D], ALU.mult))
        ch.link(dve.tensor_reduce(got.rearrange("p t h -> p (t h)"), by_head(t), AX_X, ALU.add))
        ch.link(dve.scalar_tensor_tensor(got, got, float(HD) ** -0.5, rec[:, :, 2:SREC].bitcast(F32),
                                         ALU.mult, ALU.mult))
    edge_scores(m, m.by_src(), [(m.t_kv, 1), (m.t_q, 0)], "e1", scores, maxima, attention_score, spill_from=D)
    run_maxima(m, "m1", scores, maxima)
    sum_runs(m, m.by_src(), "s2", SOFT, scores, maxima)

    def attention_out(v):
        dve, link = v.dve, v.link
        v.results_free()
        w = v.sums[:, :, D:D + H]
        link(dve.tensor_scalar(w, w, 1e-16, None, ALU.add))
        link(dve.tensor_scalar(v.buf["own"][:], w, 1e-37, None, ALU.max))
        link(dve.reciprocal(v.buf["own"][:], v.buf["own"][:]))
        for t in range(v.NB):
            last = dve.tensor_tensor(v.y[:, t, :].rearrange("p (h c) -> p h c", h=H),
                                     v.sums[:, t, 0:D].rearrange("p (h c) -> p h c", h=H),
                                     wide(v.buf["own"][:, t, :], HD), ALU.mult)
        link(last)
        turned(v)
        v.give()
        v.made()
        add_row(v, v.buf["xl"], 2, v.row[0][:])
        normalise(v, v.y[:], v.buf["xl"][:])
        link(dve.tensor_tensor(v.y[:], v.y[:], across(v.row[1][:], v.NB), ALU.mult))
        link(dve.tensor_tensor(v.y[:], v.y[:], across(v.row[2][:], v.NB), ALU.add))
        link(dve.scalar_tensor_tensor(v.x[:], v.x[:], 2.0, v.y[:], ALU.mult, ALU.add))
        normalise(v, v.y[:], v.x[:])
        turned(v)
        v.give()
        v.give()
        v.made()
        for tiles, part in pieces(v, 4):
            last = dve.tensor_copy(v.buf["xl"][:, tiles, :], part)
        link(last)
        v.made()
        for tiles, part in pieces(v, 6):
            last = dve.tensor_copy(v.buf["xr"][:, tiles, :], part)
        link(last)
        link(dve.tensor_tensor(v.tmp[:], v.buf["xl"][:], v.buf["xr"][:], ALU.add))
        link(dve.scalar_tensor_tensor(v.tmp[:], v.tmp[:], SLOPE, v.tmp[:], ALU.mult, ALU.max))
        link(dve.tensor_tensor(v.tmp[:], v.tmp[:], across(v.row[3][:], v.NB), ALU.mult))
        link(dve.tensor_reduce(flat_heads(v.buf["own"][:]), by_head(v.tmp[:]), AX_X, ALU.add))
    node_stage(m, "n3", attention_out,
               [turn_into("y", 0), times(0, 2), turn_into("y", 0), times(1, 4), times(2, 6)], [root, root],
               fetch=BY_SRC, cols=slice(0, RW), weights=[a["Wo"], a["Wl"], a["Wr"]],
               rows=[a["bo"], a["gamma"], a["beta"], a["att"]],
               buffers=[("own", H), ("xl", D), ("xr", D)],
               stores=[(m.x_now, 0, D, "y"), (m.t_xl, 0, D, "xl"), (m.t_xr, 0, D, "xr"),
                       (m.t_sdst, 0, H, "own")])

    def gatv2_score(dve, ch, row, rows, rec, tmp, got):
        t = tmp[:, 0]
        ch.link(dve.tensor_tensor(t, rows[0], rows[1], ALU.add))
        ch.link(dve.scalar_tensor_tensor(t, t, SLOPE, t, ALU.mult, ALU.max))
        ch.link(dve.tensor_tensor(t, t, across(row[0][:], STEP), ALU.mult))
        ch.link(dve.tensor_reduce(got.rearrange("p t h -> p (t h)"), by_head(t), AX_X, ALU.add))
    edge_scores(m, m.by_dst(), [(m.t_xl, 0), (m.t_xr, 1)], "e2", scores, maxima, gatv2_score, spill_from=0,
                rows=[a["att"]])
    run_maxima(m, "m2", scores, maxima)
    sum_runs(m, m.by_dst(), "s3", SOFT, scores, maxima)
    guard.__exit__(None, None, None)
    nc.all_engine_barrier()

    def gatv2_out(v):
        dve, link = v.dve, v.link
        v.results_free()
        e = v.buf["e"]
        mx = v.sums[:, :, D + H:RW]
        link(dve.tensor_scalar(v.small[:, 0, :], v.mask[:], -LOW, LOW, ALU.mult, ALU.add))
        link(dve.tensor_tensor(mx, mx, wide(v.small[:, 0, :], H), ALU.add))
        link(dve.tensor_tensor(e[:, :, 2 * H:3 * H], mx, v.buf["own"][:], ALU.max))
        link(dve.tensor_tensor(e[:, :, 0:H], mx, e[:, :, 2 * H:3 * H], ALU.subtract))
        link(dve.tensor_tensor(e[:, :, H:2 * H], v.buf["own"][:], e[:, :, 2 * H:3 * H], ALU.subtract))
        v.ask()
        link(dve.tensor_tensor(e[:, :, 2 * H:3 * H], v.sums[:, :, D:D + H], e[:, :, 0:H], ALU.mult))
        link(dve.tensor_tensor(e[:, :, 2 * H:3 * H], e[:, :, 2 * H:3 * H], e[:, :, H:2 * H], ALU.add))
        link(dve.reciprocal(e[:, :, 2 * H:3 * H], e[:, :, 2 * H:3 * H]))
        link(dve.tensor_tensor(e[:, :, 0:H], e[:, :, 0:H], e[:, :, 2 * H:3 * H], ALU.mult))
        link(dve.tensor_tensor(e[:, :, H:2 * H], e[:, :, H:2 * H], e[:, :, 2 * H:3 * H], ALU.mult))
        for src, k, dst in ((v.sums, 0, v.y), (v.buf["xl"], 1, v.tmp)):
            for t in range(v.NB):
                last = dve.tensor_tensor(dst[:, t, :].rearrange("p (h c) -> p h c", h=H),
                                         src[:, t, 0:D].rearrange("p (h c) -> p h c", h=H),
                                         wide(e[:, t, k * H:(k + 1) * H], HD), ALU.mult)
            link(last)
        link(dve.tensor_tensor(v.y[:], v.y[:], v.tmp[:], ALU.add))
        link(dve.tensor_tensor(v.y[:], v.y[:], across(v.row[0][:], v.NB), ALU.add))
        link(dve.tensor_scalar(v.tmp[:], v.y[:], 0.0, None, ALU.min))
        v.ask()
        link(dve.tensor_scalar(v.y[:], v.y[:], 0.0, -1.0, ALU.max, ALU.add))
        link(dve.tensor_tensor(v.y[:], v.y[:], v.tmp[:], ALU.add))
        link(dve.tensor_tensor(v.x[:], v.x[:], v.y[:], ALU.add))
        normalise(v, v.y[:], v.x[:])
        turned(v)
        v.give()
        v.made()
        for tiles, part in pieces(v, 2):
            last = dve.tensor_copy(v.buf["h"][:, tiles, :], part)
        link(last)

    def exp_e(v, act):
        return act.activation(v.buf["e"][:, :, 0:2 * H], v.buf["e"][:, :, 0:2 * H], ACT.Exp)

    def exp_tmp(v, act):
        return act.activation(v.tmp[:], v.tmp[:], ACT.Exp)
    node_stage(m, "n4", gatv2_out, [turn_into("y", 0), times(0, 2)], [exp_e, exp_tmp, root],
               fetch=BY_DST, cols=slice(0, RW), weights=[a["W_in"]], rows=[a["bias"]],
               buffers=[("own", H), ("xl", D), ("e", 3 * H), ("h", D)],
               stores=[(m.x_now, 0, D, "y"), (m.t_h3, 0, D, "h")],
               also=[("own", m.t_sdst), ("xl", m.t_xl)])

    sum_runs(m, m.by_dst(), "s4", FILTER)

    def last_layer(v):
        dve, link = v.dve, v.link
        v.results_free()
        link(dve.tensor_copy(v.y[:], v.sums[:, :, 0:D]))
        turned(v)
        v.give()
        v.made()
        add_row(v, v.y, 2, v.row[0][:])
        v.ask()
        turned(v)
        v.give()
        v.made()
        add_row(v, v.y, 2, v.row[1][:])
        link(dve.tensor_tensor(v.x[:], v.x[:], v.y[:], ALU.add))
        normalise(v, v.y[:], v.x[:])

    def tanh_y(v, act):
        return act.activation(v.y[:], v.y[:], ACT.Tanh)
    node_stage(m, "n5", last_layer, [turn_into("y", 0), times(0, 2), turn_into("y", 0), times(1, 2)],
               [tanh_y, root], fetch=BY_DST, cols=slice(0, D), weights=[a["W_out"], a["W_lin"]],
               rows=[a["b_out"], a["b_lin"]], stores=[(out, 0, D, "y")])



def kernel(**inputs):
    import concourse.bacc as bacc
    from concourse.bass_utils import run_bass_kernel_spmd

    x = np.asarray(inputs["x"])
    src, dst = np.asarray(inputs["src"]), np.asarray(inputs["dst"])
    N, E = x.shape[0], src.shape[0]
    G = -(-E // (P * CHUNKS))
    T = CHUNKS * G
    NB = 7
    NT = -(-(-(-(N + 1) // P)) // NB) * NB

    def pad(a, n, value=0):
        return np.concatenate([a, np.full((n - a.shape[0], *a.shape[1:]), value, a.dtype)])

    def tiled(a):
        a = a.reshape(CHUNKS, G, P, *a.shape[1:])
        return np.ascontiguousarray(a.transpose(2, 1, 0, *range(3, a.ndim)))

    rec = np.stack([pad(src, T * P, N), pad(dst, T * P, N)], axis=1)
    attr = pad(np.asarray(inputs["edge_attr_50"]), T * P).reshape(CHUNKS, G, P, -1)
    xp = pad(x, NT * P)
    arrays = {
        "x": xp, "xT": np.ascontiguousarray(xp.T),
        "rec_by_dst": tiled(rec).reshape(P, T * 2),
        "edge_attr_8": tiled(pad(np.asarray(inputs["edge_attr_8"]), T * P)).reshape(P, T * H),
        "edge_weight": tiled(pad(np.asarray(inputs["edge_weight"]), T * P)).reshape(P, T),
        "edge_attr_50": np.ascontiguousarray(attr.transpose(3, 1, 0, 2)).reshape(-1, T * P),
        "src_attn": np.asarray(inputs["L0_gnn_src_attn"]).reshape(-1),
        "dst_attn": np.asarray(inputs["L0_gnn_dst_attn"]).reshape(-1),
        "att": np.asarray(inputs["L2_gnn_att"]).reshape(-1),
        "W": inputs["L0_gnn_W"],
    }
    for name in ("Wq", "bq", "Wk", "bk", "Wv", "bv", "Wo", "bo", "gamma", "beta"):
        arrays[name] = inputs[f"L1_gnn_{name}"]
    for name in ("Wl", "Wr", "bias"):
        arrays[name] = inputs[f"L2_gnn_{name}"]
    for name in ("W_f1", "b_f1", "W_f2", "b_f2", "W_in", "W_out", "b_out", "W_lin", "b_lin"):
        arrays[name] = inputs[f"L3_gnn_{name}"]
    arrays = {f"in_{k}": np.ascontiguousarray(v) for k, v in arrays.items()}

    nc = bacc.Bacc("TRN2", target_bir_lowering=False, num_devices=1)
    args = {k[3:]: nc.dram_tensor(k, v.shape, mybir.dt.from_np(v.dtype), kind="ExternalInput").ap()
            for k, v in arrays.items()}
    out = nc.dram_tensor("out", (NT * P, D), F32, kind="ExternalOutput").ap()
    build(nc, args, out, N, G, NB)
    r = run_bass_kernel_spmd(nc, [arrays], core_ids=[0])
    return r.results[0]["out"][:N]
```

```python
import numpy as np

import concourse.bass as bass
from concourse import mybir

F32 = mybir.dt.float32
BF16 = mybir.dt.bfloat16
I32 = mybir.dt.int32
ALU = mybir.AluOpType
ACT = mybir.ActivationFunctionType
AX_X = mybir.AxisListType.X

P = 128
D = 128
H = 8
HD = D // H
CHUNKS = 16
STEP = 4
SLOTS = CHUNKS // STEP
RW = D + 2 * H
LOW = -1.0e30
EPS = 1e-5
SLOPE = 0.2
CUTOFF = 10.0
PI = float(np.pi)



def wide(ap, n):
    return ap.unsqueeze(len(ap.shape)).to_broadcast([*ap.shape, n])


def across(ap, n):
    return ap.unsqueeze(1).to_broadcast([ap.shape[0], n, *ap.shape[1:]])


class Chain:

    def __init__(self, eng, sem):
        self.eng, self.sem, self.start, self.n = eng, sem, 0, 0

    def link(self, ins):
        ins.then_inc(self.sem, 1)
        self.n += 1
        self.eng.wait_ge(self.sem, self.start + self.n)

    def turn(self, g):
        if isinstance(g, int) and g == 0:
            self.outer, self.n, self.per = self.start + self.n, 0, None
            self.start = self.outer
        else:
            self.per = self.per or self.n
            self.start, self.n = g * self.per + self.outer, 0

    def leave(self, turns):
        self.start, self.n = self.outer + turns * (self.per or self.n), 0


def turns(eng, count, body):
    body(0, True)
    if count > 1:
        with eng.Fori(1, count) as g:
            body(g, False)


def turns_ahead(eng, count, body):
    body(0, True, count == 1)
    if count > 2:
        with eng.Fori(1, count - 1) as g:
            body(g, False, False)
    if count > 1:
        body(count - 1, False, True)


class Machine:

    def __init__(self, nc, args, N, G, NB):
        self.nc, self.args, self.G, self.NB = nc, args, G, NB
        self.T = CHUNKS * G
        self.F = G * P
        self.NT = -(-(-(-(N + 1) // P)) // NB) * NB
        self.NP = self.NT * P
        self.NI = self.NT // NB

        def dram(name, shape, dt=F32):
            return nc.dram_tensor(name, shape, dt).ap()
        T, NP = self.T, self.NP
        self.rec_by_src = dram("rec_by_src", (P * T, SREC), I32)
        self.sums = {n: dram(f"sums{n}", (T * P, n)) for n in (2 * H, D, RW)}
        self.spill = dram("spill", (G * SLOTS * P, STEP * D))
        self.x_now = dram("x_now", (NP, D))
        self.t_ssrc = dram("t_ssrc", (NP, H))
        self.t_own = dram("t_own", (NP, H))
        self.t_gat = dram("t_gat", (NP, D + 3 * H))
        self.c_ssrc = dram("c_ssrc", (NP, H + 1))
        self.c_sdst = dram("c_sdst", (NP, H + 1))
        self.c_q = dram("c_q", (NP, D + 1))
        self.c_xr = dram("c_xr", (NP, D + 1))
        self.compact = [dram(f"compact{w}", (NP, 1), I32) for w in range(2)]
        self.window_row = dram("window_row", (T, 1), I32)
        self.t_kv = dram("t_kv", (NP, 2 * D))
        self.t_xl = dram("t_xl", (NP, D))
        self.t_h3 = dram("t_h3", (NP, D))
        self.chunk_ends = dram("chunk_ends", (P, 2))
        self.chunk_carry = dram("chunk_carry", (P + H, 1))

        sb = nc.alloc_sbuf_tensor
        self.ps = nc.alloc_psum_tensor("ps", [P, 8, 512], F32)
        self.ident = sb("ident", [P, P], F32)
        self.ident16 = sb("ident16", [P, P], BF16)
        self.lane = sb("lane", [P, 1], F32)
        self.column = sb("column", [P, P], F32)
        self.only_last = sb("only_last", [P, 2], F32)
        self.last_rank = sb("last_rank", [P, 2, self.NT], F32)
        self.first_rank = sb("first_rank", [P, 2, self.NT], F32)
        self.last_index = sb("last_index", [P, 2, self.NT], I32)
        self.compact_index = sb("compact_index", [P, 2, self.NT], I32)
        self.node_id = sb("node_id", [P, self.NT], F32)
        self.window_start = sb("window_start", [1, 2, T], I32)

    def by_dst(self):
        return self.args["rec_by_dst"], 2, 1, 0

    def by_src(self):
        return self.rec_by_src.rearrange("(p t) c -> p (t c)", p=P), SREC, 0, 1


SREC = H + 2
BY_SRC, BY_DST = 0, 1


class stage:

    def __init__(self, m, name):
        self.m, self.name = m, name

    def __enter__(self):
        self.guard = self.m.nc.cleanup_on_exit()
        self.guard.__enter__()
        return self

    def __exit__(self, *a):
        self.guard.__exit__(*a)
        self.m.nc.all_engine_barrier()

    def sem(self, name):
        return self.m.nc.alloc_semaphore(f"{self.name}_{name}")

    def sems(self, name, n=SLOTS):
        return [self.sem(f"{name}{b}") for b in range(n)]

    def sb(self, name, shape, dt=F32):
        return self.m.nc.alloc_sbuf_tensor(f"{self.name}_{name}", shape, dt)


def ahead(b, g, n, last):
    if last and b + n >= SLOTS:
        return None
    return (b + n) % SLOTS, g + (b + n) // SLOTS


def hold(eng, sem, n, spare):
    eng.wait_ge(sem, n)
    eng.sem_inc(spare, 1)


def take(dve, out, data):
    return dve.tensor_scalar(out, data, 0.0, None, ALU.add)


def constants(m):
    nc = m.nc
    with stage(m, "const") as s:
        counted, chain = s.sem("counted"), s.sem("chain")
        with nc.Block() as block:
            @block.gpsimd
            def _(pool):
                pool.iota(m.lane[:], [[0, 1]], base=0, channel_multiplier=1,
                          allow_small_or_imprecise_dtypes=True).then_inc(counted, 1)
                pool.iota(m.column[:], [[1, P]], base=0, channel_multiplier=0,
                          allow_small_or_imprecise_dtypes=True).then_inc(counted, 1)

            @block.vector
            def _(dve):
                ch = Chain(dve, chain)
                dve.wait_ge(counted, 2)
                ch.link(dve.tensor_scalar(m.ident[:], m.column[:], m.lane[:, 0:1], None, ALU.is_equal))
                ch.link(dve.tensor_scalar(m.ident16[:], m.column[:], m.lane[:, 0:1], None, ALU.is_equal))
                ch.link(dve.tensor_scalar(m.only_last[:, 0:1], m.lane[:], float(P - 1), None, ALU.is_equal))
                ch.link(dve.tensor_scalar(m.only_last[:, 1:2], m.only_last[:, 0:1], 1.0, None, ALU.subtract))
                ch.link(dve.tensor_scalar(m.node_id[:], m.column[:, 0:m.NT], float(P), m.lane[:, 0:1],
                                          ALU.mult, ALU.add))



def count_edges(m, which, first_ranks):
    nc, T, NT, ps = m.nc, m.T, m.NT, m.ps
    U = 8
    field = 0 if which == BY_SRC else 1
    with stage(m, f"count{which}") as s:
        rec = s.sb("rec", [P, T, 2], I32)
        hi_i = s.sb("hi_i", [P, T], I32)
        idf, hi, lo = (s.sb(n, [P, T]) for n in ("idf", "hi", "lo"))
        hot_hi = s.sb("hot_hi", [P, 2, U, NT], BF16)
        hot_lo = s.sb("hot_lo", [P, 2, U, P], BF16)
        zero = s.sb("zero", [P, P], BF16)
        one = s.sb("one", [P, P])
        hist, last, before = (s.sb(n, [P, P]) for n in ("hist", "last", "before"))
        has, place, ids, other = (s.sb(n, [P, P]) for n in ("has", "place", "ids", "other"))
        place_i = s.sb("place_i", [P, P], I32)
        total, ahead = s.sb("total", [P, 2]), s.sb("ahead", [P, 3])
        place_out = s.sem("place_out")
        rec_in, chain = s.sem("rec_in"), s.sem("chain")
        hots_ready, hots_used = s.sem("hots_ready"), s.sem("hots_used")
        zero_ready, hist_ready, total_ready = s.sem("zero_ready"), s.sem("hist_ready"), s.sem("total_ready")
        ahead_ready, ranks_ready, ranks_turned = s.sem("ahead_ready"), s.sem("ranks_ready"), s.sem("ranks_turned")
        assert T % (2 * U) == 0
        turns = T // (2 * U)
        with nc.Block() as block:
            @block.sync
            def _(sp):
                sp.dma_start(rec[:].rearrange("p t c -> p (t c)"), m.args["rec_by_dst"]).then_inc(rec_in, 16)
                sp.wait_ge(ranks_ready, 1)
                sp.dma_start(m.compact[which].rearrange("(h l) c -> h (l c)", l=P), place_i[0:NT, :]
                             ).then_inc(place_out, 16)
                sp.wait_ge(place_out, 16)

            @block.vector
            def _(dve):
                ch = Chain(dve, chain)
                ch.link(dve.memset(one[:], 1.0))
                dve.memset(zero[:], 0.0).then_inc(zero_ready, 1)
                dve.wait_ge(rec_in, 16)
                ch.link(dve.tensor_copy(idf[:], rec[:, :, field]))
                ch.link(dve.tensor_scalar(hi_i[:], rec[:, :, field], 7, None, ALU.logical_shift_right))
                ch.link(dve.tensor_copy(hi[:], hi_i[:]))
                ch.link(dve.scalar_tensor_tensor(lo[:], hi[:], float(-P), idf[:], ALU.mult, ALU.add))
                dve.sem_inc(hots_used, 2)
                with dve.Fori(0, turns) as c:
                    for k in range(2):
                        dve.wait_ge(hots_used, c * 2 + k + 1)
                        at = bass.ds(c * (2 * U) + k * U, U)
                        dve.tensor_tensor(hot_hi[:, k], across(m.column[:, 0:NT], U), wide(hi[:, at], NT),
                                          ALU.is_equal)
                        dve.tensor_tensor(hot_lo[:, k], across(m.column[:], U), wide(lo[:, at], P),
                                          ALU.is_equal).then_inc(hots_ready, 1)
                dve.wait_ge(hist_ready, 1)
                ch.link(dve.tensor_copy(hist[0:NT, :], ps[0:NT, 0, 0:P]))
                ch.link(dve.tensor_tensor_scan(last[0:NT, :], one[0:NT, :], hist[0:NT, :], 0.0,
                                               ALU.mult, ALU.add))
                ch.link(dve.tensor_copy(total[0:NT, 0:1], last[0:NT, P - 1:P]))
                ch.link(dve.tensor_scalar(has[0:NT, :], hist[0:NT, :], 0.0, None, ALU.is_gt))
                ch.link(dve.tensor_tensor_scan(place[0:NT, :], one[0:NT, :], has[0:NT, :], 0.0,
                                               ALU.mult, ALU.add))
                ch.link(dve.tensor_copy(total[0:NT, 1:2], place[0:NT, P - 1:P]))
                dve.tensor_scalar(before[0:NT, :], m.column[0:NT, :], m.lane[0:NT, 0:1], None,
                                  ALU.is_gt).then_inc(total_ready, 1)
                dve.wait_ge(ahead_ready, 1)
                ch.link(dve.tensor_copy(ahead[0:NT, :], ps[0:NT, 1, 0:3]))
                ch.link(dve.tensor_scalar(place[0:NT, :], place[0:NT, :], ahead[0:NT, 1:2], None, ALU.add))
                ch.link(dve.tensor_scalar(ids[0:NT, :], m.lane[0:NT, 0:1].to_broadcast([NT, P]), float(P), None,
                                          ALU.mult))
                ch.link(dve.tensor_tensor(ids[0:NT, :], ids[0:NT, :], m.column[0:NT, :], ALU.add))
                ch.link(dve.scalar_tensor_tensor(other[0:NT, :], ids[0:NT, :], ahead[0:NT, 2:3], place[0:NT, :],
                                                 ALU.add, ALU.subtract))
                ch.link(dve.tensor_scalar(place[0:NT, :], place[0:NT, :], -1.0, None, ALU.add))
                ch.link(dve.tensor_tensor(place[0:NT, :], place[0:NT, :], other[0:NT, :], ALU.subtract))
                ch.link(dve.tensor_tensor(place[0:NT, :], place[0:NT, :], has[0:NT, :], ALU.mult))
                ch.link(dve.tensor_tensor(place[0:NT, :], place[0:NT, :], other[0:NT, :], ALU.add))
                ch.link(dve.tensor_copy(place_i[0:NT, :], place[0:NT, :]))
                ch.link(dve.tensor_scalar(last[0:NT, :], last[0:NT, :], ahead[0:NT, 0:1], None, ALU.add))
                ch.link(dve.tensor_tensor(first_ranks[0:NT, :], last[0:NT, :], hist[0:NT, :], ALU.subtract))
                dve.tensor_scalar(last[0:NT, :], last[0:NT, :], -1.0, None, ALU.add).then_inc(ranks_ready, 1)
                dve.wait_ge(ranks_turned, 1)
                ch.link(dve.tensor_copy(m.last_rank[:, which, :], ps[:, 2, 0:NT]))
                ch.link(dve.tensor_copy(m.first_rank[:, which, :], ps[:, 3, 0:NT]))
                ch.link(dve.tensor_copy(m.compact_index[:, which, :], ps[:, 4, 0:NT]))
                ch.link(dve.tensor_copy(m.last_index[:, which, :], m.last_rank[:, which, :]))

            @block.tensor
            def _(pe):
                pe.wait_ge(zero_ready, 1)
                pe.matmul(ps[0:NT, 0, 0:P], zero[:, 0:NT], zero[:], start=True, stop=False)
                with pe.Fori(0, turns) as c:
                    for k in range(2):
                        pe.wait_ge(hots_ready, c * 2 + k + 1)
                        for u in range(U):
                            ins = pe.matmul(ps[0:NT, 0, 0:P], hot_hi[:, k, u, :], hot_lo[:, k, u, :],
                                            start=False, stop=False)
                        ins.then_inc(hots_used, 1)
                pe.matmul(ps[0:NT, 0, 0:P], zero[:, 0:NT], zero[:], start=False, stop=True,
                          ).then_inc(hist_ready, 1)
                pe.wait_ge(total_ready, 1)
                pe.matmul(ps[0:NT, 1, 0:2], before[0:NT, 0:NT], total[0:NT, :], start=True, stop=True)
                pe.matmul(ps[0:NT, 1, 2:3], one[0:NT, 0:NT], total[0:NT, 1:2], start=True,
                          stop=True).then_inc(ahead_ready, 1)
                pe.wait_ge(ranks_ready, 1)
                pe.transpose(ps[:, 2, 0:NT], last[0:NT, :], m.ident[0:NT, 0:NT])
                pe.transpose(ps[:, 4, 0:NT], place[0:NT, :], m.ident[0:NT, 0:NT])
                pe.transpose(ps[:, 3, 0:NT], first_ranks[0:NT, :], m.ident[0:NT, 0:NT]).then_inc(ranks_turned, 1)


def tile_windows(m, which, order):
    nc, T, NP = m.nc, m.T, m.NP
    rec_dram, rw, seg, _ = order
    whole, rest = T // P, T % P
    with stage(m, f"windows{which}") as s:
        first = s.sb("first", [P, whole + 1], I32)
        start = s.sb("start", [P, whole + 1], I32)
        moved, clamped, gathered = s.sem("moved"), s.sem("clamped"), s.sem("gathered")
        cuts = [(0, P, i) for i in range(whole)] + ([(whole, rest, whole)] if rest else [])
        with nc.Block() as block:
            def columns(flat, sb):
                both = [(flat[0:whole * P, :].rearrange("(i p) c -> p i c", p=P), sb[:, 0:whole].unsqueeze(2))]
                if rest:
                    both.append((flat[whole * P:T, :].rearrange("(i p) c -> p i c", p=rest),
                                 sb[0:rest, whole:whole + 1].unsqueeze(2)))
                return both
            n = 16 * len(columns(m.window_row, first))

            @block.sync
            def _(sp):
                for flat, sb in columns(rec_dram[0:1, :].rearrange("o (t c) -> (o t) c", c=rw)[:, seg:seg + 1],
                                        first):
                    sp.dma_start(sb, flat, allow_slow_non_contiguous=True).then_inc(moved, 16)
                sp.wait_ge(clamped, 1)
                for flat, sb in columns(m.window_row, start):
                    sp.dma_start(flat, sb, allow_slow_non_contiguous=True).then_inc(moved, 16)
                sp.wait_ge(moved, 2 * n)
                sp.dma_start(m.window_start[:, which, :], m.window_row.rearrange("t c -> c t")).then_inc(moved, 16)
                sp.wait_ge(moved, 2 * n + 16)

            @block.gpsimd
            def _(pool):
                pool.wait_ge(moved, n)
                for _, parts, i in cuts:
                    pool.indirect_dma_start(
                        out=start[0:parts, i:i + 1], out_offset=None, in_=m.compact[which],
                        in_offset=bass.IndirectOffsetOnAxis(ap=first[0:parts, i:i + 1], axis=0)
                    ).then_inc(gathered, 16)

            @block.vector
            def _(dve):
                dve.wait_ge(gathered, 16 * len(cuts))
                if whole:
                    last = dve.tensor_scalar(start[:, 0:whole], start[:, 0:whole], float(NP - P), None, ALU.min)
                if rest:
                    last = dve.tensor_scalar(start[0:rest, whole:], start[0:rest, whole:], float(NP - P), None,
                                             ALU.min)
                last.then_inc(clamped, 1)


def load_windows(m, sp, table, which, step, win, landed):
    at = m.window_start[:, which, bass.ds(step * STEP, STEP)]
    _, starts = m.nc.values_load_multi_w_load_instructions(
        at, engines=(sp.engine,), min_val=0, max_val=m.NP - P,
        skip_runtime_bounds_check_because="tile_windows clamps the starts")
    for t in range(STEP):
        sp.dma_start(win[:, t, :], table[bass.ds(starts[t], P), :]).then_inc(landed, 16)


def sort_by_src(m, next_rank):
    nc, T, G, NT, ps = m.nc, m.T, m.G, m.NT, m.ps
    with stage(m, "sort") as s:
        rec = s.sb("rec", [P, T, 2], I32)
        hi_i = s.sb("hi_i", [P, T], I32)
        idf, hi, lo = (s.sb(n, [P, T]) for n in ("idf", "hi", "lo"))
        id_now = s.sb("id_now", [P, 2, STEP])
        earlier = s.sb("earlier", [P, P])
        chunk_tile = s.sb("chunk_tile", [P, CHUNKS])
        weight = s.sb("weight", [P, SLOTS, STEP * H])
        hot_hi = s.sb("hot_hi", [P, 2, STEP, NT], BF16)
        hot_lo = s.sb("hot_lo", [P, 2, STEP, P], BF16)
        hiT = s.sb("hiT", [P, 2, STEP * P])
        same = s.sb("same", [P, 2 * STEP, STEP * P])
        part = s.sb("part", [P, 3, CHUNKS])
        rank = s.sb("rank", [P, CHUNKS])
        rank_i, tile_i = s.sb("rank_i", [P, CHUNKS], I32), s.sb("tile_i", [P, CHUNKS], I32)
        tile_no, chunk, pos = (s.sb(n, [P, CHUNKS]) for n in ("tile_no", "chunk", "pos"))
        past = s.sb("past", [P, CHUNKS, CHUNKS])
        pos_i = s.sb("pos_i", [P, CHUNKS], I32)
        rec_out = s.sb("rec_out", [P, CHUNKS, SREC], I32)
        rec_in, chain, spare, sent = s.sem("rec_in"), s.sem("chain"), s.sem("spare"), s.sem("sent")
        weight_in = s.sems("weight_in")
        (hots_ready, rows_ready, hiT_ready, hiT_kept, looked_up, counted, next_ready, picked, places_ready,
         weights_ready) = (s.sem(n) for n in (
             "hots_ready", "rows_ready", "hiT_ready", "hiT_kept", "looked_up", "counted", "next_ready",
             "picked", "places_ready", "weights_ready"))

        def steps(g, last):
            for b in range(SLOTS):
                yield b, g * SLOTS + b, not (last and b == SLOTS - 1)

        with nc.Block() as block:
            @block.sync
            def _(sp):
                sp.dma_start(rec[:].rearrange("p t c -> p (t c)"), m.args["rec_by_dst"]).then_inc(rec_in, 16)

                def turn(g, first):
                    for b in range(SLOTS):
                        if not first:
                            sp.wait_ge(weights_ready, (g - 1) * SLOTS + b + 1)
                        sp.dma_start(weight[:, b],
                                     m.args["edge_attr_8"][:, bass.ds((g * SLOTS + b) * (STEP * H), STEP * H)]
                                     ).then_inc(weight_in[b], 16)
                turns(sp, G, turn)

            @block.gpsimd
            def _(pool):
                def turn(g, first):
                    hold(pool, weights_ready, (g + 1) * SLOTS, spare)
                    hold(pool, places_ready, g + 1, spare)
                    for t in range(CHUNKS):
                        pool.indirect_dma_start(
                            out=m.rec_by_src,
                            out_offset=bass.IndirectOffsetOnAxis(ap=pos_i[:, t:t + 1], axis=0),
                            in_=rec_out[:, t, :], in_offset=None).then_inc(sent, 16)
                turns(pool, G, turn)
                pool.wait_ge(sent, 16 * CHUNKS * G)

            @block.scalar
            def _(act):
                def keep_hiT(b, k):
                    act.wait_ge(hiT_ready, k + 1)
                    act.activation(hiT[0:NT, b % 2, :], ps[0:NT, 2 + b % 2, :], ACT.Copy).then_inc(hiT_kept, 1)

                def turn(g, first, last):
                    if first:
                        keep_hiT(0, 0)
                    for b, k, more in steps(g, last):
                        act.wait_ge(counted, k + 1)
                        act.activation(next_rank[0:NT, :], ps[0:NT, 5, 0:P], ACT.Copy).then_inc(next_ready, 1)
                        if more:
                            keep_hiT(b + 1, k + 1)
                    if not first:
                        act.wait_ge(sent, g * (16 * CHUNKS))
                    for b in range(SLOTS):
                        act.wait_ge(weight_in[b], (g + 1) * 16)
                        act.activation(rec_out[:, b * STEP:(b + 1) * STEP, 2:SREC].bitcast(F32),
                                       weight[:, b].rearrange("p (t c) -> p t c", c=H), ACT.Copy
                                       ).then_inc(weights_ready, 1)
                turns_ahead(act, G, turn)

            @block.tensor
            def _(pe):
                def turn_ids(b, k, early):
                    if not early:
                        pe.wait_ge(picked, k - 1)
                    pe.wait_ge(hots_ready, k + 1)
                    for t in range(STEP):
                        ins = pe.matmul(ps[0:NT, 2 + b % 2, t * P:(t + 1) * P], hot_hi[:, b % 2, t, :],
                                        m.ident16[:], start=True, stop=True)
                    ins.then_inc(hiT_ready, 1)
                    for t in range(STEP):
                        ins = pe.transpose(ps[:, b % 2, t * P:(t + 1) * P],
                                           id_now[:, b % 2, t:t + 1].to_broadcast([P, P]), m.ident[:])
                    ins.then_inc(rows_ready, 1)

                def turn(g, first, last):
                    if first:
                        turn_ids(0, 0, True)
                    for b, k, more in steps(g, last):
                        pe.wait_ge(hiT_kept, k + 1)
                        if not (first and b == 0):
                            pe.wait_ge(next_ready, k)
                        if not (first and b < 2):
                            pe.wait_ge(picked, k - 1)
                        for t in range(STEP):
                            ins = pe.matmul(ps[:, 6 + b % 2, t * P:(t + 1) * P],
                                            hiT[0:NT, b % 2, t * P:(t + 1) * P],
                                            next_rank[0:NT, :], start=True, stop=True)
                        ins.then_inc(looked_up, 1)
                        pe.matmul(ps[0:NT, 5, 0:P], m.ident[0:NT, 0:NT], next_rank[0:NT, :], start=True, stop=False)
                        for t in range(STEP):
                            ins = pe.matmul(ps[0:NT, 5, 0:P], hot_hi[:, b % 2, t, :], hot_lo[:, b % 2, t, :],
                                            start=False, stop=t == STEP - 1)
                        ins.then_inc(counted, 1)
                        if more:
                            turn_ids(b + 1, k + 1, first and b < 1)
                turns_ahead(pe, G, turn)

            @block.vector
            def _(dve):
                ch = Chain(dve, chain)
                dve.wait_ge(rec_in, 16)
                ch.link(dve.tensor_copy(idf[:], rec[:, :, 0]))
                ch.link(dve.tensor_scalar(hi_i[:], rec[:, :, 0], 7, None, ALU.logical_shift_right))
                ch.link(dve.tensor_copy(hi[:], hi_i[:]))
                ch.link(dve.scalar_tensor_tensor(lo[:], hi[:], float(-P), idf[:], ALU.mult, ALU.add))
                ch.link(dve.tensor_scalar(earlier[:], m.column[:], m.lane[:, 0:1], None, ALU.is_lt))
                ch.link(dve.memset(part[:], 0.0))
                ch.link(dve.tensor_scalar(chunk_tile[:], m.column[:, 0:CHUNKS], float(G), None, ALU.mult))

                def hots(b, k, early):
                    if not early:
                        dve.wait_ge(counted, k - 1)
                    at = bass.ds(k * STEP, STEP)
                    take(dve, id_now[:, b % 2, :], idf[:, at])
                    dve.tensor_tensor(hot_hi[:, b % 2], across(m.column[:, 0:NT], STEP), wide(hi[:, at], NT),
                                      ALU.is_equal)
                    dve.tensor_tensor(hot_lo[:, b % 2], across(m.column[:], STEP), wide(lo[:, at], P),
                                      ALU.is_equal).then_inc(hots_ready, 1)

                def turn(g, first, last):
                    ch.turn(g)
                    if first:
                        hots(0, 0, True)
                    for b, k, more in steps(g, last):
                        if more:
                            hots(b + 1, k + 1, first and b < 1)
                        dve.wait_ge(rows_ready, k + 1)
                        for t in range(STEP):
                            c = b * STEP + t
                            col = id_now[:, b % 2, t:t + 1]
                            if t:
                                dve.tensor_scalar(same[:, t, 0:t * P], ps[:, b % 2, 0:t * P], col, 0.0,
                                                  ALU.is_equal, ALU.add, accum_out=part[:, 1, c:c + 1])
                            last_op = dve.scalar_tensor_tensor(
                                same[:, 0, t * P:(t + 1) * P], ps[:, b % 2, t * P:(t + 1) * P], col, earlier[:],
                                ALU.is_equal, ALU.mult, accum_out=part[:, 0, c:c + 1])
                        ch.link(last_op)
                        dve.wait_ge(looked_up, k + 1)
                        for t in range(STEP):
                            c = b * STEP + t
                            last_op = dve.scalar_tensor_tensor(
                                same[:, STEP + t, 0:P], ps[:, 6 + b % 2, t * P:(t + 1) * P], 1.0,
                                hot_lo[:, b % 2, t, :], ALU.mult, ALU.mult, accum_out=part[:, 2, c:c + 1])
                        last_op.then_inc(picked, 1)
                        dve.wait_ge(picked, k + 1)
                    ch.link(dve.tensor_tensor(rank[:], part[:, 0, :], part[:, 2, :], ALU.add))
                    ch.link(dve.tensor_tensor(rank[:], rank[:], part[:, 1, :], ALU.add))
                    ch.link(dve.tensor_copy(rank_i[:], rank[:]))
                    ch.link(dve.tensor_scalar(tile_i[:], rank_i[:], 7, None, ALU.logical_shift_right))
                    ch.link(dve.tensor_copy(tile_no[:], tile_i[:]))
                    dve.tensor_tensor(past[:], wide(tile_no[:], CHUNKS), across(chunk_tile[:], CHUNKS), ALU.is_ge)
                    ch.link(dve.scalar_tensor_tensor(pos[:], tile_no[:], float(-P), rank[:], ALU.mult, ALU.add))
                    ch.link(dve.tensor_reduce(chunk[:], past[:], AX_X, ALU.add))
                    ch.link(dve.tensor_scalar(pos[:], pos[:], float(T), float(CHUNKS * G - 1), ALU.mult, ALU.add))
                    ch.link(dve.scalar_tensor_tensor(pos[:], tile_no[:], float(CHUNKS), pos[:], ALU.mult, ALU.add))
                    if not first:
                        dve.wait_ge(sent, g * (16 * CHUNKS))
                    ch.link(take(dve, rec_out[:, :, 0:2], rec[:, bass.ds(g * CHUNKS, CHUNKS), :]))
                    dve.scalar_tensor_tensor(pos_i[:], chunk[:], float(1 - CHUNKS * G), pos[:],
                                             ALU.mult, ALU.add).then_inc(places_ready, 1)
                turns_ahead(dve, G, turn)



def edge_scores(m, order, which, table, width, windows, name, scores, maxima, score_of, spill_from=None,
                rows=()):
    nc, G, ps = m.nc, m.G, m.ps
    rec_dram, rw, seg, other = order
    own_width = windows.shape[1] - 1
    with stage(m, name) as s:
        rec = s.sb("rec", [P, SLOTS, STEP, rw], I32)
        got_rows = s.sb("got_rows", [P, SLOTS, STEP, width])
        win = s.sb("win", [P, SLOTS, STEP, own_width + 1])
        segs = s.sb("segs", [P, SLOTS, STEP])
        onehot = s.sb("onehot", [P, 2, STEP, P])
        tmp = s.sb("tmp", [P, STEP, D])
        got = s.sb("got", [P, CHUNKS, H])
        ids = s.sb("ids", [P, CHUNKS, H])
        row_sb = [s.sb(f"row{n}", [P, r.shape[0]]) for n, r in enumerate(rows)]
        rec_in, win_in, gathered, spilled = (s.sems(n) for n in ("rec_in", "win_in", "gathered", "spilled"))
        rows_in, chain, spare = s.sem("rows_in"), s.sem("chain"), s.sem("spare")
        segs_ready, rows_ready, onehot_ready, expanded = (s.sem(n) for n in (
            "segs_ready", "rows_ready", "onehot_ready", "expanded"))
        step_done, group_ready, turned, kept = (s.sem(n) for n in ("step_done", "group_ready", "turned", "kept"))
        with nc.Block() as block:
            @block.sync
            def _(sp):
                for sb_row, r in zip(row_sb, rows):
                    sp.dma_start(sb_row[:], r.unsqueeze(0).to_broadcast([P, r.shape[0]])).then_inc(rows_in, 16)

                def turn(g, first):
                    for b in range(SLOTS):
                        if not first:
                            sp.wait_ge(step_done, (g - 1) * SLOTS + b + 1)
                        sp.dma_start(rec[:, b].rearrange("p t c -> p (t c)"),
                                     rec_dram[:, bass.ds((g * SLOTS + b) * (STEP * rw), STEP * rw)]
                                     ).then_inc(rec_in[b], 16)
                        load_windows(m, sp, windows, which, g * SLOTS + b, win[:, b], win_in[b])
                turns(sp, G, turn)

            @block.gpsimd
            def _(pool):
                def turn(g, first):
                    for b in range(SLOTS):
                        hold(pool, rec_in[b], (g + 1) * 16, spare)
                        if spill_from is not None and not first:
                            hold(pool, spilled[b], g * 16, spare)
                        for t in range(STEP):
                            pool.indirect_dma_start(
                                out=got_rows[:, b, t, :], out_offset=None, in_=table,
                                in_offset=bass.IndirectOffsetOnAxis(ap=rec[:, b, t, other:other + 1], axis=0),
                            ).then_inc(gathered[b], 16)
                turns(pool, G, turn)

            @block.scalar
            def _(act):
                def number(b, g):
                    act.wait_ge(rec_in[b], (g + 1) * 16)
                    act.activation(segs[:, b, :], rec[:, b, :, seg], ACT.Copy).then_inc(segs_ready, 1)

                def turn(g, first, last):
                    if first:
                        number(0, 0)
                        number(1, 0)
                    for b in range(SLOTS):
                        if ahead(b, g, 2, last):
                            number(*ahead(b, g, 2, last))
                        if spill_from is not None:
                            act.wait_ge(gathered[b], (g + 1) * (16 * STEP))
                            act.dma_start(
                                m.spill[bass.ds((g * SLOTS + b) * P, P), :].rearrange("p (t c) -> p t c", t=STEP),
                                got_rows[:, b, :, spill_from:spill_from + D]).then_inc(spilled[b], 16)
                    hold(act, turned, g + 1, spare)
                    at = bass.ds(g * P, P)
                    act.activation(scores[:, at], ps[:, 0, 0:P], ACT.Copy)
                    act.activation(maxima[:, at], ps[:, 0, P:2 * P], ACT.Copy).then_inc(kept, 1)
                turns_ahead(act, G, turn)
                if spill_from is not None:
                    for b in range(SLOTS):
                        act.wait_ge(spilled[b], 16 * G)

            @block.tensor
            def _(pe):
                def id_rows(b, g, early):
                    k = g * SLOTS + b
                    if not early:
                        pe.wait_ge(onehot_ready, k - 1)
                    pe.wait_ge(segs_ready, k + 1)
                    for t in range(STEP):
                        ins = pe.transpose(ps[:, 1 + b % 2, t * P:(t + 1) * P],
                                           segs[:, b, t:t + 1].to_broadcast([P, P]), m.ident[:])
                    ins.then_inc(rows_ready, 1)

                def expand(b, g, early):
                    k = g * SLOTS + b
                    if not early:
                        pe.wait_ge(step_done, k - 1)
                    pe.wait_ge(onehot_ready, k + 1)
                    for t in range(STEP):
                        ins = pe.matmul(ps[:, 3 + b % 2, t * own_width:(t + 1) * own_width],
                                        onehot[:, b % 2, t, :], win[:, b, t, 0:own_width],
                                        start=True, stop=True)
                    ins.then_inc(expanded, 1)

                def turn(g, first, last):
                    if first:
                        id_rows(0, 0, True)
                        id_rows(1, 0, True)
                        expand(0, 0, True)
                    for b in range(SLOTS):
                        if ahead(b, g, 2, last):
                            id_rows(*ahead(b, g, 2, last), False)
                        if ahead(b, g, 1, last):
                            expand(*ahead(b, g, 1, last), first and b < 1)
                    if not first:
                        pe.wait_ge(kept, g)
                    pe.wait_ge(group_ready, g + 1)
                    pe.transpose(ps[:, 0, 0:P], got[:].rearrange("p j h -> p (j h)"), m.ident[:])
                    pe.transpose(ps[:, 0, P:2 * P], ids[:].rearrange("p j h -> p (j h)"),
                                 m.ident[:]).then_inc(turned, 1)
                turns_ahead(pe, G, turn)

            @block.vector
            def _(dve):
                ch = Chain(dve, chain)
                if rows:
                    dve.wait_ge(rows_in, 16 * len(rows))

                def one_hots(b, g, early):
                    k = g * SLOTS + b
                    dve.wait_ge(win_in[b], (g + 1) * (16 * STEP))
                    if not early:
                        dve.wait_ge(expanded, k - 1)
                    dve.wait_ge(rows_ready, k + 1)
                    dve.tensor_tensor(onehot[:, b % 2], ps[:, 1 + b % 2, :].rearrange("p (t c) -> p t c", c=P),
                                      wide(win[:, b, :, own_width], P), ALU.is_equal
                                      ).then_inc(onehot_ready, 1)

                def turn(g, first, last):
                    ch.turn(g)
                    if first:
                        one_hots(0, 0, True)
                    for b in range(SLOTS):
                        k = g * SLOTS + b
                        if ahead(b, g, 1, last):
                            one_hots(*ahead(b, g, 1, last), first and b < 1)
                        if b == 0 and not first:
                            dve.wait_ge(turned, g)
                        dve.wait_ge(gathered[b], (g + 1) * (16 * STEP))
                        dve.wait_ge(expanded, k + 1)
                        dve.tensor_copy(ids[:, b * STEP:(b + 1) * STEP, :], wide(segs[:, b, :], H))
                        own = ps[:, 3 + b % 2, 0:STEP * own_width].rearrange("p (t c) -> p t c", c=own_width)
                        score_of(dve, ch, row_sb, got_rows[:, b], own, rec[:, b], tmp,
                                 got[:, b * STEP:(b + 1) * STEP, :])
                        dve.sem_inc(step_done, 1)
                    dve.sem_inc(group_ready, 1)
                turns_ahead(dve, G, turn)
                ch.leave(G)


def run_maxima(m, name, scores, maxima, totals=False):
    nc, F, ps = m.nc, m.F, m.ps
    with stage(m, name) as s:
        starts = s.sb("starts", [P, F + 1], BF16)
        bound = s.sb("bound", [P, 2])
        ends = s.sb("ends", [P, 2])
        carried = s.sb("carried", [P, 1])
        line = s.sb("line", [H, CHUNKS, 2])
        linked = s.sb("linked", [H, CHUNKS])
        low = s.sb("low", [H, 1])
        moved, chain, give, diff, weighed = (s.sem(n) for n in ("moved", "chain", "give", "diff", "weighed"))
        PIECES = 4
        cuts = [F * i // PIECES for i in range(PIECES + 1)]
        with nc.Block() as block:
            @block.sync
            def _(sp):
                sp.wait_ge(give, 1)
                sp.dma_start(bound[H:P, 0:1], maxima[0:P - H, F - 1:F]).then_inc(moved, 16)
                sp.dma_start(bound[0:P - H, 1:2], maxima[H:P, 0:1]).then_inc(moved, 16)
                sp.wait_ge(moved, 32)
                for way in range(2):
                    sp.wait_ge(give, 2 + 2 * way)
                    sp.dma_start(m.chunk_ends, ends[:]).then_inc(moved, 16)
                    sp.wait_ge(moved, 32 + way * 80 + 16)
                    sp.dma_start(line[:], m.chunk_ends.rearrange("(j h) c -> h j c", h=H)).then_inc(moved, 16)
                    sp.wait_ge(moved, 32 + way * 80 + 32)
                    sp.wait_ge(give, 3 + 2 * way)
                    carry = m.chunk_carry.rearrange("(j h) c -> h j c", h=H)
                    if way == 0:
                        sp.dma_start(carry[:, 1:CHUNKS + 1, :], linked[:].unsqueeze(2),
                                     allow_slow_non_contiguous=True).then_inc(moved, 16)
                        sp.dma_start(carry[:, 0:1, :], low[:].unsqueeze(2),
                                     allow_slow_non_contiguous=True).then_inc(moved, 16)
                    else:
                        sp.dma_start(carry[:, 0:CHUNKS, :], linked[:].unsqueeze(2),
                                     allow_slow_non_contiguous=True).then_inc(moved, 16)
                        sp.dma_start(carry[:, CHUNKS:CHUNKS + 1, :], low[:].unsqueeze(2),
                                     allow_slow_non_contiguous=True).then_inc(moved, 16)
                    sp.wait_ge(moved, 32 + way * 80 + 64)
                    first = 0 if way == 0 else H
                    sp.dma_start(carried[:], m.chunk_carry[first:first + P, :]).then_inc(moved, 16)
                    sp.wait_ge(moved, 32 + way * 80 + 80)

            @block.vector
            def _(dve):
                ch = Chain(dve, chain)
                ch.link(dve.memset(low[:], LOW))
                dve.memset(bound[:], -1.0).then_inc(give, 1)
                dve.wait_ge(moved, 32)
                dve.tensor_tensor(starts[:, 1:F], maxima[:, 1:F], maxima[:, 0:F - 1], ALU.not_equal)
                dve.tensor_tensor(starts[:, 0:1], maxima[:, 0:1], bound[:, 0:1], ALU.not_equal)
                ch.link(dve.tensor_tensor(starts[:, F:F + 1], maxima[:, F - 1:F], bound[:, 1:2], ALU.not_equal))
                ch.link(dve.tensor_scalar(starts[:], starts[:], LOW, None, ALU.mult))
                back = maxima[:, ::-1]
                for way in range(2):
                    flags = starts[:, 0:F] if way == 0 else starts[:, 1:F + 1]
                    end = F - 1 if way == 0 else 0

                    def scan(initial):
                        if way == 0:
                            return dve.tensor_tensor_scan(maxima[:], flags, scores[:], initial, ALU.add, ALU.max)
                        return dve.tensor_tensor_scan(back, starts[:, F:0:-1], back, initial, ALU.add, ALU.max)
                    ch.link(scan(LOW))
                    ch.link(dve.tensor_copy(ends[:, 0:1], maxima[:, end:end + 1]))
                    dve.tensor_reduce(ends[:, 1:2], flags, AX_X, ALU.min).then_inc(give, 1)
                    dve.wait_ge(moved, 32 + way * 80 + 32)
                    if way == 0:
                        dve.tensor_tensor_scan(linked[:], line[:, :, 1], line[:, :, 0], LOW,
                                               ALU.add, ALU.max).then_inc(give, 1)
                    else:
                        dve.tensor_tensor_scan(linked[:, ::-1], line[:, ::-1, 1], line[:, ::-1, 0], LOW,
                                               ALU.add, ALU.max).then_inc(give, 1)
                    dve.wait_ge(moved, 32 + way * 80 + 80)
                    ch.link(scan(carried[:, 0:1]))
                for a, z in zip(cuts, cuts[1:]):
                    dve.tensor_tensor(scores[:, a:z], scores[:, a:z], maxima[:, a:z], ALU.subtract
                                      ).then_inc(diff, 1)
                if totals:
                    ch.link(dve.tensor_scalar(starts[:], starts[:], 0.0, None, ALU.is_equal))
                    dve.wait_ge(weighed, PIECES)
                    dve.tensor_tensor_scan(scores[:], starts[:, 0:F], scores[:], 0.0, ALU.mult, ALU.add)

            @block.scalar
            def _(act):
                for n, (a, z) in enumerate(zip(cuts, cuts[1:])):
                    act.wait_ge(diff, n + 1)
                    act.activation(scores[:, a:z], scores[:, a:z], ACT.Exp).then_inc(weighed, 1)


def totals_by_rank(m, name, scores, maxima):
    nc, G, ps = m.nc, m.G, m.ps
    U = 2 if G % 2 == 0 else 1
    with stage(m, name) as s:
        by_run = s.sb("by_run", [P, U, 2, P])
        both = s.sb("both", [P, U, CHUNKS, 2, H])
        apart, turned, kept = (s.sem(n) for n in ("apart", "turned", "kept"))
        stored = s.sems("stored", U)
        with nc.Block() as block:
            @block.vector
            def _(dve):
                def turn(g, first):
                    for u in range(U):
                        k = g * U + u
                        at = bass.ds(k * P, P)
                        if not first:
                            dve.wait_ge(turned, k - U + 1)
                        take(dve, by_run[:, u, 0, :], scores[:, at])
                        take(dve, by_run[:, u, 1, :], maxima[:, at]).then_inc(apart, 1)
                turns(dve, G // U, turn)

            @block.tensor
            def _(pe):
                def turn(g, first):
                    for u in range(U):
                        k = g * U + u
                        if not first:
                            pe.wait_ge(kept, k - U + 1)
                        pe.wait_ge(apart, k + 1)
                        pe.transpose(ps[:, u, 0:P], by_run[:, u, 0, :], m.ident[:])
                        pe.transpose(ps[:, u, P:2 * P], by_run[:, u, 1, :], m.ident[:]).then_inc(turned, 1)
                turns(pe, G // U, turn)

            @block.scalar
            def _(act):
                def turn(g, first):
                    for u in range(U):
                        k = g * U + u
                        act.wait_ge(turned, k + 1)
                        if not first:
                            act.wait_ge(stored[u], g * 16)
                        act.activation(both[:, u], ps[:, u, 0:2 * P].rearrange("p (a j h) -> p j a h", a=2, h=H),
                                       ACT.Copy).then_inc(kept, 1)
                        act.wait_ge(kept, k + 1)
                        act.dma_start(
                            m.sums[2 * H].rearrange("(j g p) c -> p g j c", g=G, p=P)[:, bass.ds(k, 1), :, :],
                            both[:, u].rearrange("p j a h -> p j (a h)").unsqueeze(1)).then_inc(stored[u], 16)
                turns(act, G // U, turn)
                for u in range(U):
                    act.wait_ge(stored[u], 16 * (G // U))



GAT, SOFT, FILTER = "gat", "soft", "filter"


def sum_runs(m, order, name, kind, scores=None, maxima=None):
    nc, G, T, ps, args = m.nc, m.G, m.T, m.ps, m.args
    rec_dram, rw, seg, other = order
    msg_cols = {GAT: slice(0, D), SOFT: slice(0, D + H), FILTER: slice(0, D)}[kind]
    out_cols = {GAT: slice(0, D), SOFT: slice(0, RW), FILTER: slice(0, D)}[kind]
    width = msg_cols.stop - msg_cols.start
    table = {GAT: m.t_gat, FILTER: m.t_h3}[kind] if kind in (GAT, FILTER) else None
    weighted = kind == SOFT
    with stage(m, name) as s:
        rec = s.sb("rec", [P, SLOTS, STEP, rw], I32)
        if table is not None:
            got_rows = s.sb("got_rows", [P, SLOTS, STEP, table.shape[1]])
        if kind == SOFT:
            kept_rows = s.sb("kept_rows", [P, SLOTS, STEP, D])
        segs = s.sb("segs", [P, CHUNKS])
        carry_id = s.sb("carry_id", [P, SLOTS, STEP])
        same = s.sb("same", [P, 2, STEP, P])
        goes_on = s.sb("goes_on", [P, 2, STEP, P])
        msg = s.sb("msg", [P, 2, STEP, D + H])
        run = s.sb("run", [P, CHUNKS, RW])
        if weighted:
            by_run = s.sb("by_run", [P, 2, P])
            pm = s.sb("pm", [P, 2, CHUNKS, H])
        if kind == GAT:
            coef = s.sb("coef", [P, 2, STEP, H])
            win = s.sb("win", [P, SLOTS, STEP, H + 1])
            onehot = s.sb("onehot", [P, 2, STEP, P])
        if kind == FILTER:
            attr = s.sb("attr", [args["W_f1"].shape[0], SLOTS, STEP * P])
            w1, w2 = s.sb("w1", list(args["W_f1"].shape)), s.sb("w2", [D, D])
            b1, b2 = s.sb("b1", [D, 1]), s.sb("b2", [P, D])
            cut, whole = s.sb("cut", [P, T]), s.sb("whole", [P, T])
            hidden = s.sb("hidden", [D, 2, STEP * P])
            filt = s.sb("filt", [P, STEP, D])
        rec_in, gathered, stored, kept_in, attr_in, win_in = (s.sems(n) for n in (
            "rec_in", "gathered", "stored", "kept_in", "attr_in", "win_in"))
        (chain, spare, step_done, segs_ready, rows_ready, sel_ready, msg_ready, summed, evacuated, turned,
         pm_ready, coef_ready, exp_ready, const_in, half_ready, cut_ready, hid_sum, hid_ready, filt_ready,
         apart, onehot_ready, expanded) = (s.sem(n) for n in (
             "chain", "spare", "step_done", "segs_ready", "rows_ready", "sel_ready", "msg_ready", "summed",
             "evacuated", "turned", "pm_ready", "coef_ready", "exp_ready", "const_in", "half_ready", "cut_ready",
             "hid_sum", "hid_ready", "filt_ready", "apart", "onehot_ready", "expanded"))

        AHEAD = 2 if kind == GAT else 1

        def sums_of(b):
            if kind == SOFT:
                return ps[:, 2 + 2 * (b % 2):4 + 2 * (b % 2), :].rearrange("p b (u c) -> p b u c", u=2)
            return ps[:, 2 + b % 2, :].rearrange("p (b u c) -> p b u c", b=2, u=2)

        with nc.Block() as block:
            @block.sync
            def _(sp):
                if kind == FILTER:
                    sp.dma_start(w1[:], args["W_f1"]).then_inc(const_in, 16)
                    sp.dma_start(w2[:], args["W_f2"]).then_inc(const_in, 16)
                    sp.dma_start(b1[:], args["b_f1"].unsqueeze(1)).then_inc(const_in, 16)
                    sp.dma_start(b2[:], args["b_f2"].unsqueeze(0).to_broadcast([P, D])).then_inc(const_in, 16)
                    sp.dma_start(cut[:], args["edge_weight"]).then_inc(const_in, 16)

                def store(b, g):
                    tiles = slice(b * STEP, (b + 1) * STEP)
                    sp.wait_ge(evacuated, g * SLOTS + b + 1)
                    sp.dma_start(
                        m.sums[out_cols.stop - out_cols.start].rearrange("(j g p) c -> p g j c", g=G, p=P)[
                            :, bass.ds(g, 1), tiles, :],
                        run[:, tiles, out_cols].unsqueeze(1)).then_inc(stored[b], 16)

                def turn(g, first):
                    for b in range(SLOTS):
                        if not first:
                            sp.wait_ge(step_done, (g - 1) * SLOTS + b + 1)
                        sp.dma_start(rec[:, b].rearrange("p t c -> p (t c)"),
                                     rec_dram[:, bass.ds((g * SLOTS + b) * (STEP * rw), STEP * rw)]
                                     ).then_inc(rec_in[b], 16)
                        if kind == GAT:
                            load_windows(m, sp, m.c_ssrc, BY_SRC, g * SLOTS + b, win[:, b], win_in[b])
                        if kind == SOFT:
                            sp.dma_start(kept_rows[:, b].rearrange("p t c -> p (t c)"),
                                         m.spill[bass.ds((g * SLOTS + b) * P, P), :]).then_inc(kept_in[b], 16)
                        if kind == FILTER:
                            if not first:
                                sp.wait_ge(hid_sum, (g - 1) * SLOTS + b + 1)
                            sp.dma_start(attr[:, b, :],
                                         args["edge_attr_50"][:, bass.ds((g * SLOTS + b) * (STEP * P), STEP * P)]
                                         ).then_inc(attr_in[b], 16)
                        if not first:
                            store(b, g - 1)
                turns(sp, G, turn)
                for b in range(SLOTS):
                    store(b, G - 1)
                for b in range(SLOTS):
                    sp.wait_ge(stored[b], 16 * G)

            if table is not None:
                @block.gpsimd
                def _(pool):
                    def turn(g, first):
                        for b in range(SLOTS):
                            hold(pool, rec_in[b], (g + 1) * 16, spare)
                            for t in range(STEP):
                                pool.indirect_dma_start(
                                    out=got_rows[:, b, t, :], out_offset=None, in_=table,
                                    in_offset=bass.IndirectOffsetOnAxis(ap=rec[:, b, t, other:other + 1], axis=0)
                                ).then_inc(gathered[b], 16)
                    turns(pool, G, turn)

            @block.tensor
            def _(pe):
                if kind == FILTER:
                    pe.wait_ge(const_in, 80)

                def id_rows(b, g, early):
                    k = g * SLOTS + b
                    if not early:
                        pe.wait_ge(sel_ready, k - 1)
                    pe.wait_ge(segs_ready, k + 1)
                    for t in range(STEP):
                        j = b * STEP + t
                        ins = pe.transpose(ps[:, b % 2, t * P:(t + 1) * P],
                                           segs[:, j:j + 1].to_broadcast([P, P]), m.ident[:])
                    ins.then_inc(rows_ready, 1)

                def hidden_sums(b, g):
                    pe.wait_ge(attr_in[b], (g + 1) * 16)
                    pe.matmul(ps[:, 6 + b % 2, :], w1[:], attr[:, b, :], start=True, stop=True
                              ).then_inc(hid_sum, 1)

                def filters(b, g):
                    pe.wait_ge(hid_ready, g * SLOTS + b + 1)
                    for t in range(STEP):
                        ins = pe.matmul(ps[:, 4 + b % 2, t * P:(t + 1) * P], hidden[:, b % 2, t * P:(t + 1) * P],
                                        w2[:], start=True, stop=True)
                    ins.then_inc(filt_ready, 1)

                def expand(b, g):
                    pe.wait_ge(onehot_ready, g * SLOTS + b + 1)
                    for t in range(STEP):
                        ins = pe.matmul(ps[:, 6 + b % 2, t * H:(t + 1) * H], onehot[:, b % 2, t, :],
                                        win[:, b, t, 0:H], start=True, stop=True)
                    ins.then_inc(expanded, 1)

                def turn_weights(g):
                    pe.wait_ge(apart, g + 1)
                    pe.transpose(ps[:, 6, 0:P], by_run[:, 0, :], m.ident[:])
                    pe.transpose(ps[:, 6, P:2 * P], by_run[:, 1, :], m.ident[:]).then_inc(turned, 1)

                def turn(g, first, last):
                    if first:
                        if weighted:
                            turn_weights(0)
                        for n in range(AHEAD):
                            id_rows(n, 0, True)
                        if kind == GAT:
                            expand(0, 0)
                        if kind == FILTER:
                            hidden_sums(0, 0)
                            hidden_sums(1, 0)
                            filters(0, 0)
                    for b in range(SLOTS):
                        k = g * SLOTS + b
                        if weighted and b == 2 and not last:
                            pe.wait_ge(pm_ready, g + 1)
                            turn_weights(g + 1)
                        if ahead(b, g, AHEAD, last):
                            id_rows(*ahead(b, g, AHEAD, last), first and b + AHEAD < 2)
                        if kind == FILTER and ahead(b, g, 1, last):
                            filters(*ahead(b, g, 1, last))
                        if kind == FILTER and ahead(b, g, 2, last):
                            hidden_sums(*ahead(b, g, 2, last))
                        if kind == GAT and ahead(b, g, 1, last):
                            expand(*ahead(b, g, 1, last))
                        if not (first and b < 2):
                            pe.wait_ge(evacuated, k - 1)
                        pe.wait_ge(sel_ready, k + 1)
                        pe.wait_ge(msg_ready, k + 1)
                        for t in range(STEP):
                            part = sums_of(b)[:, t // 2, t % 2, 0:width]
                            pe.matmul(part, same[:, b % 2, t, :], msg[:, b % 2, t, msg_cols],
                                      start=True, stop=False)
                            ins = pe.matmul(part, goes_on[:, b % 2, t, :], run[:, b * STEP + t, msg_cols],
                                            start=False, stop=True)
                        ins.then_inc(summed, 1)
                turns_ahead(pe, G, turn)

            @block.scalar
            def _(act):
                if kind == FILTER:
                    act.wait_ge(const_in, 80)
                    act.wait_ge(half_ready, 1)
                    act.activation(cut[:], cut[:], ACT.Sin, scale=PI).then_inc(cut_ready, 1)

                def hide(b, g):
                    act.wait_ge(hid_sum, g * SLOTS + b + 1)
                    act.activation(hidden[:, b % 2, :], ps[:, 6 + b % 2, :], ACT.Tanh, bias=b1[:, 0:1]
                                   ).then_inc(hid_ready, 1)

                def weigh(b, g):
                    act.wait_ge(coef_ready, g * SLOTS + b + 1)
                    act.activation(coef[:, b % 2], coef[:, b % 2], ACT.Exp).then_inc(exp_ready, 1)

                def set_apart(g):
                    at = bass.ds(g * P, P)
                    act.activation(by_run[:, 0, :], scores[:, at], ACT.Copy)
                    act.activation(by_run[:, 1, :], maxima[:, at], ACT.Copy).then_inc(apart, 1)

                def turn(g, first, last):
                    if weighted:
                        if first:
                            set_apart(0)
                        if not last:
                            act.wait_ge(turned, g + 1)
                            set_apart(g + 1)
                    if first and kind == FILTER:
                        hide(0, 0)
                        hide(1, 0)
                    if first and kind == GAT:
                        weigh(0, 0)
                    for b in range(SLOTS):
                        k = g * SLOTS + b
                        if kind == GAT and ahead(b, g, 1, last):
                            weigh(*ahead(b, g, 1, last))
                        if kind == FILTER and ahead(b, g, 2, last):
                            hide(*ahead(b, g, 2, last))
                        act.wait_ge(summed, k + 1)
                        if not first:
                            act.wait_ge(stored[b], g * 16)
                        tiles = slice(b * STEP, (b + 1) * STEP)
                        act.activation(run[:, tiles, msg_cols].rearrange("p (b u) c -> p b u c", u=2),
                                       sums_of(b)[:, :, :, 0:width], ACT.Copy).then_inc(evacuated, 1)
                turns_ahead(act, G, turn)

            @block.vector
            def _(dve):
                ch = Chain(dve, chain)
                ch.link(dve.memset(segs[:], -1.0))
                ch.link(dve.memset(run[:], 0.0))
                if kind == FILTER:
                    dve.wait_ge(const_in, 80)
                    ch.link(dve.tensor_scalar(cut[:], cut[:], 0.5 / CUTOFF, None, ALU.mult))
                    ch.link(dve.tensor_scalar(whole[:], cut[:], ROUND, None, ALU.add))
                    ch.link(dve.tensor_scalar(whole[:], whole[:], -ROUND, None, ALU.add))
                    dve.tensor_tensor(cut[:], cut[:], whole[:], ALU.subtract).then_inc(half_ready, 1)
                    dve.wait_ge(cut_ready, 1)
                    ch.link(dve.tensor_tensor(cut[:], cut[:], cut[:], ALU.mult))
                    ch.link(dve.tensor_scalar(cut[:], cut[:], -1.0, 1.0, ALU.mult, ALU.add))

                def number(b, g):
                    tiles = slice(b * STEP, (b + 1) * STEP)
                    dve.wait_ge(rec_in[b], (g + 1) * 16)
                    ch.link(dve.tensor_scalar(carry_id[:, b, :], segs[:, tiles], m.only_last[:, 0:1],
                                              m.only_last[:, 1:2], ALU.mult, ALU.add))
                    dve.tensor_copy(segs[:, tiles], rec[:, b, :, seg]).then_inc(segs_ready, 1)

                def id_rows_of(b):
                    return ps[:, b % 2, :].rearrange("p (t c) -> p t c", c=P)

                def find(b, g):
                    k = g * SLOTS + b
                    dve.wait_ge(rows_ready, k + 1)
                    dve.wait_ge(win_in[b], (g + 1) * (16 * STEP))
                    dve.tensor_tensor(onehot[:, b % 2], id_rows_of(b), wide(win[:, b, :, H], P), ALU.is_equal
                                      ).then_inc(onehot_ready, 1)

                def turn(g, first, last):
                    if first:
                        for n in range(AHEAD):
                            number(n, 0)
                        if kind == GAT:
                            find(0, 0)
                    ch.turn(g)
                    if weighted:
                        dve.wait_ge(turned, g + 1)
                        dve.tensor_copy(pm[:].rearrange("p a j h -> p (a j h)"), ps[:, 6, 0:2 * P]
                                        ).then_inc(pm_ready, 1)
                    for b in range(SLOTS):
                        k = g * SLOTS + b
                        tiles = slice(b * STEP, (b + 1) * STEP)
                        if kind == GAT:
                            rows, c = got_rows[:, b], coef[:, b % 2]
                            dve.wait_ge(gathered[b], (g + 1) * (16 * STEP))
                            dve.wait_ge(expanded, k + 1)
                            ch.link(dve.tensor_tensor(c, rows[:, :, D:D + H],
                                                      ps[:, 6 + b % 2, 0:STEP * H].rearrange("p (t h) -> p t h", h=H),
                                                      ALU.add))
                            ch.link(dve.scalar_tensor_tensor(c, c, SLOPE, c, ALU.mult, ALU.max))
                            dve.tensor_tensor(c, c, rows[:, :, D + 2 * H:D + 3 * H], ALU.subtract
                                              ).then_inc(coef_ready, 1)
                            if ahead(b, g, 1, last):
                                find(*ahead(b, g, 1, last))
                        if ahead(b, g, AHEAD, last):
                            number(*ahead(b, g, AHEAD, last))
                        dve.wait_ge(rows_ready, k + 1)
                        if not (first and b < 2):
                            dve.wait_ge(summed, k - 1)
                        dve.tensor_tensor(same[:, b % 2], id_rows_of(b), wide(segs[:, tiles], P), ALU.is_equal)
                        dve.tensor_tensor(goes_on[:, b % 2], id_rows_of(b), wide(carry_id[:, b, :], P),
                                          ALU.is_equal).then_inc(sel_ready, 1)
                        out = msg[:, b % 2]
                        if kind == GAT:
                            dve.wait_ge(exp_ready, k + 1)
                            ch.link(dve.tensor_tensor(c, c, rows[:, :, D + H:D + 2 * H], ALU.mult))
                            values, weights = rows[:, :, 0:D], c
                        if weighted:
                            dve.wait_ge(pm_ready, g + 1)
                            weights = pm[:, 0, tiles, :]
                            if not first:
                                dve.wait_ge(stored[b], g * 16)
                            dve.tensor_copy(run[:, tiles, D + H:RW], pm[:, 1, tiles, :])
                            last_op = dve.tensor_copy(out[:, :, D:D + H], weights)
                        if kind == SOFT:
                            dve.wait_ge(kept_in[b], (g + 1) * 16)
                            values = kept_rows[:, b]
                        if kind in (GAT, SOFT):
                            last_op = dve.tensor_tensor(split_heads(out[:, :, 0:D]), split_heads(values),
                                                        wide(weights, HD), ALU.mult)
                        if kind == FILTER:
                            dve.wait_ge(filt_ready, k + 1)
                            dve.wait_ge(gathered[b], (g + 1) * (16 * STEP))
                            ch.link(dve.tensor_tensor(filt[:], ps[:, 4 + b % 2, :].rearrange("p (t c) -> p t c", c=D),
                                                      across(b2[:], STEP), ALU.add))
                            for t in range(STEP):
                                last_op = dve.scalar_tensor_tensor(
                                    out[:, t, 0:D], filt[:, t, :], cut[:, bass.ds(k * STEP + t, 1)],
                                    got_rows[:, b, t, :], ALU.mult, ALU.mult)
                        last_op.then_inc(msg_ready, 1)
                        dve.wait_ge(msg_ready, k + 1)
                        dve.sem_inc(step_done, 1)
                turns_ahead(dve, G, turn)


ROUND = 1.5 * 2.0 ** 23



class BlockView:
    pass


def node_stage(m, name, steps, products, asks=(), fetch=None, cols=None, weights=(), rows=(), features=None,
               turned_in=None, buffers=(), stores=(), also=(), scatters=()):
    nc, NB, NI, F, ps = m.nc, m.NB, m.NI, m.F, m.ps
    with stage(m, name) as s:
        v = BlockView()
        v.m, v.s, v.ps, v.NB = m, s, ps, NB
        v.x = s.sb("x", [P, NB, D])
        v.y = s.sb("y", [P, NB, D])
        v.tmp = s.sb("tmp", [P, NB, D])
        v.yT = s.sb("yT", [P, NB * P])
        v.small = s.sb("small", [P, 2, NB])
        v.row = [s.sb(f"row{n}", [P, r.shape[0]]) for n, r in enumerate(rows)]
        v.w = [s.sb(f"w{n}", [P, w.shape[1]]) for n, w in enumerate(weights)]
        v.buf = {n: s.sb(n, [P, NB, width]) for n, width in buffers}
        v.buf["y"] = v.y
        const_in, chain, spare, x_in, stored, block_done = (s.sem(n) for n in (
            "const_in", "chain", "spare", "x_in", "stored", "block_done"))
        given, made, asked, answered, idx_ready, fetched = (s.sem(n) for n in (
            "given", "made", "asked", "answered", "idx_ready", "fetched"))
        pe_steps = list(products)
        to_place = [s.sb(f"place{n}", [P, NB], I32) for n in range(len(scatters))]
        placed = s.sem("placed")
        if fetch is not None:
            sums = m.sums[cols.stop - cols.start]
            got = s.sb("got", [P, NB, RW])
            v.sums = s.sb("sums", [P, NB, RW])
            idx = s.sb("idx", [P, NB], I32)
            cross, before = s.sb("cross", [P, NB, CHUNKS]), s.sb("before", [P, NB, CHUNKS])
            crossT = s.sb("crossT", [CHUNKS, NB * P])
            tails = s.sb("tails", [CHUNKS, RW])
            tail_rank = s.sb("tail_rank", [P, CHUNKS])
            v.mask = s.sb("mask", [P, NB])

            def turn_cross(pe):
                for t in range(NB):
                    ins = pe.transpose(ps[0:CHUNKS, t // 4, (t % 4) * P:(t % 4 + 1) * P], cross[:, t, :],
                                       m.ident[:])
                return ins

            def add_tails(pe):
                for t in range(NB):
                    ins = pe.matmul(ps[:, 2 + t // 3, (t % 3) * RW:(t % 3) * RW + cols.stop - cols.start],
                                    crossT[:, t * P:(t + 1) * P], tails[:, cols], start=True, stop=True)
                return ins
            pe_steps = [turn_cross, add_tails] + pe_steps
        n_const = 16 * (len(weights) + len(rows) + (fetch is not None))
        NPROD, NASK = len(pe_steps), len(asks)

        def block_rows(table, g, a, z):
            return table[bass.ds(g * (NB * P), NB * P), a:z].rearrange("(t p) c -> p t c", p=P)

        with nc.Block() as block:
            @block.sync
            def _(sp):
                for w, d in zip(v.w, weights):
                    sp.dma_start(w[:], d).then_inc(const_in, 16)
                for r, d in zip(v.row, rows):
                    sp.dma_start(r[:], d.unsqueeze(0).to_broadcast([P, d.shape[0]])).then_inc(const_in, 16)
                if fetch is not None:
                    sp.dma_start(tails[:, cols], sums.rearrange("(j f) c -> j f c", f=F)[:, F - 1, :]
                                 ).then_inc(const_in, 16)

                def turn(g, first):
                    if not first:
                        sp.wait_ge(block_done, g)
                    if turned_in is not None:
                        sp.dma_start(v.yT[:], turned_in[:, bass.ds(g * (NB * P), NB * P)]).then_inc(x_in, 16)
                    else:
                        sp.dma_start(v.x[:], block_rows(features if features is not None else m.x_now, g, 0, D)
                                     ).then_inc(x_in, 16)
                    for n, table in also:
                        sp.dma_start(v.buf[n][:], block_rows(table, g, 0, table.shape[1])).then_inc(x_in, 16)
                turns(sp, NI, turn)

            if fetch is not None or scatters:
                @block.gpsimd
                def _(pool):
                    def fetch_sums(g):
                        hold(pool, idx_ready, g + 1, spare)
                        for t in range(NB):
                            pool.indirect_dma_start(
                                out=got[:, t, cols], out_offset=None, in_=sums,
                                in_offset=bass.IndirectOffsetOnAxis(ap=idx[:, t:t + 1], axis=0)
                            ).then_inc(fetched, 16)

                    def turn(g, first, last):
                        if fetch is not None:
                            if first:
                                fetch_sums(0)
                            if not last:
                                fetch_sums(g + 1)
                        if scatters:
                            hold(pool, block_done, g + 1, spare)
                            for n, (table, _, name_of) in enumerate(scatters):
                                for t in range(NB):
                                    pool.indirect_dma_start(
                                        out=table,
                                        out_offset=bass.IndirectOffsetOnAxis(ap=to_place[n][:, t:t + 1], axis=0),
                                        in_=v.buf[name_of][:, t, :], in_offset=None).then_inc(placed, 16)
                    turns_ahead(pool, NI, turn)
                    if scatters:
                        pool.wait_ge(placed, 16 * NB * len(scatters) * NI)

            @block.tensor
            def _(pe):
                pe.wait_ge(const_in, n_const)

                def turn(g, first):
                    for n, product in enumerate(pe_steps):
                        pe.wait_ge(given, g * NPROD + n + 1)
                        ins = product(pe) if (fetch is not None and n < 2) else product(v, pe)
                        ins.then_inc(made, 1)
                turns(pe, NI, turn)

            @block.scalar
            def _(act):
                def turn(g, first):
                    for n, ask in enumerate(asks):
                        act.wait_ge(asked, g * NASK + n + 1)
                        ask(v, act).then_inc(answered, 1)
                    act.wait_ge(block_done, g + 1)
                    for table, a, z, name_of in stores:
                        act.dma_start(block_rows(table, g, a, z), v.buf[name_of][:, :, 0:z - a]
                                      ).then_inc(stored, 16)
                turns(act, NI, turn)
                act.wait_ge(stored, 16 * len(stores) * NI)

            @block.vector
            def _(dve):
                ch = Chain(dve, chain)
                v.dve, v.link = dve, ch.link
                dve.wait_ge(const_in, n_const) if n_const else None
                if fetch is not None:
                    ch.link(dve.tensor_scalar(tail_rank[:], m.column[:, 0:CHUNKS], float(F), float(F - 1),
                                              ALU.mult, ALU.add))

                def place_last(g):
                    ch.link(dve.tensor_scalar(idx[:], m.last_index[:, fetch, bass.ds(g * NB, NB)], 0.0, None,
                                              ALU.max))
                    dve.sem_inc(idx_ready, 1)

                if fetch is not None:
                    place_last(0)

                def turn(g, first, last):
                    ch.turn(g)
                    v.g, count = g, {"made": 0, "answered": 0}

                    def give():
                        dve.sem_inc(given, 1)

                    def made_wait():
                        count["made"] += 1
                        dve.wait_ge(made, g * NPROD + count["made"])

                    def ask():
                        dve.sem_inc(asked, 1)
                        count["answered"] += 1
                        dve.wait_ge(answered, g * NASK + count["answered"])

                    def results_free():
                        if not first:
                            dve.wait_ge(stored, g * (16 * len(stores)))
                            if scatters:
                                dve.wait_ge(placed, g * (16 * NB * len(scatters)))
                        at = bass.ds(g * NB, NB)
                        for n, (_, which, name_of) in enumerate(scatters):
                            width = v.buf[name_of].shape[2]
                            ch.link(take(dve, to_place[n][:], m.compact_index[:, which, at]))
                            ch.link(take(dve, v.buf[name_of][:, :, width - 1], m.node_id[:, at]))
                    v.give, v.made, v.ask, v.results_free = give, made_wait, ask, results_free
                    if fetch is not None:
                        at = bass.ds(g * NB, NB)
                        lr, fr = m.last_rank[:, fetch, at], m.first_rank[:, fetch, at]
                        dve.tensor_tensor(v.mask[:], lr, fr, ALU.is_ge)
                        dve.tensor_tensor(cross[:], across(tail_rank[:], NB), wide(fr, CHUNKS), ALU.is_ge)
                        ch.link(dve.tensor_tensor(before[:], across(tail_rank[:], NB), wide(lr, CHUNKS),
                                                  ALU.is_lt))
                        ch.link(dve.tensor_tensor(cross[:], cross[:], before[:], ALU.mult))
                        give()
                        made_wait()
                        for a in range(0, NB, 4):
                            n = min(4, NB - a) * P
                            last_op = dve.tensor_copy(crossT[:, a * P:a * P + n], ps[0:CHUNKS, a // 4, 0:n])
                        ch.link(last_op)
                        give()
                        dve.wait_ge(fetched, (g + 1) * (16 * NB))
                        ch.link(dve.tensor_tensor(v.sums[:, :, cols], got[:, :, cols],
                                                  wide(v.mask[:], cols.stop - cols.start), ALU.mult))
                        if not last:
                            place_last(g + 1)
                        made_wait()
                        added = slice(cols.start, min(cols.stop, D + H))
                        for a in range(0, NB, 3):
                            n = min(3, NB - a)
                            part = ps[:, 2 + a // 3, 0:n * RW].rearrange("p (t c) -> p t c", c=RW)
                            last_op = dve.tensor_tensor(v.sums[:, a:a + n, added], v.sums[:, a:a + n, added],
                                                        part[:, :, 0:added.stop - added.start], ALU.add)
                        ch.link(last_op)
                    dve.wait_ge(x_in, (g + 1) * (16 * (1 + len(also))))
                    steps(v)
                    assert count["made"] == NPROD and count["answered"] == NASK, (count, NPROD, NASK)
                    dve.sem_inc(block_done, 1)
                turns_ahead(dve, NI, turn)


def pieces(v, bank):
    return [(slice(a, min(a + 4, v.NB)),
             v.ps[:, bank + a // 4, 0:(min(a + 4, v.NB) - a) * P].rearrange("p (t c) -> p t c", c=P))
            for a in range(0, v.NB, 4)]


def turn_into(src, bank):
    def product(v, pe):
        for t in range(v.NB):
            ins = pe.transpose(v.ps[:, bank + t // 4, (t % 4) * P:(t % 4 + 1) * P],
                               v.buf[src][:, t, :], v.m.ident[:])
        return ins
    return product


def times(w, bank):
    def product(v, pe):
        for t in range(v.NB):
            ins = pe.matmul(v.ps[:, bank + t // 4, (t % 4) * P:(t % 4 + 1) * P], v.yT[:, t * P:(t + 1) * P],
                            v.w[w][:], start=True, stop=True)
        return ins
    return product


def turned(v):
    v.give()
    v.made()
    for tiles, part in pieces(v, 0):
        last = v.dve.tensor_copy(v.yT[:, tiles.start * P:tiles.stop * P], part.rearrange("p t c -> p (t c)"))
    v.link(last)


def add_row(v, out, bank, row):
    for tiles, part in pieces(v, bank):
        last = v.dve.tensor_tensor(out[:, tiles, :], part, across(row, tiles.stop - tiles.start), ALU.add)
    v.link(last)


def normalise(v, out, x):
    dve, link = v.dve, v.link
    mean, var = v.small[:, 0, :], v.small[:, 1, :]
    link(dve.tensor_reduce(mean, x, AX_X, ALU.add))
    link(dve.tensor_scalar(mean, mean, 1.0 / D, None, ALU.mult))
    link(dve.tensor_tensor(out, x, wide(mean, D), ALU.subtract))
    link(dve.tensor_tensor(v.tmp[:], out, out, ALU.mult))
    link(dve.tensor_reduce(var, v.tmp[:], AX_X, ALU.add))
    link(dve.tensor_scalar(var, var, 1.0 / D, EPS, ALU.mult, ALU.add))
    v.ask()
    link(dve.reciprocal(var, var))
    link(dve.tensor_tensor(out, out, wide(var, D), ALU.mult))


def root(v, act):
    return act.activation(v.small[:, 1, :], v.small[:, 1, :], ACT.Sqrt)


def by_head(ap):
    return ap.rearrange("p t (h c) -> p (t h) c", h=H)


def split_heads(ap):
    return ap.rearrange("p t (h c) -> p t h c", h=H)


def flat_heads(ap):
    return ap.rearrange("p t h -> p (t h)")



def build(nc, args, out, N, G, NB):
    m = Machine(nc, args, N, G, NB)
    constants(m)
    a = args

    next_rank = nc.alloc_sbuf_tensor("next_rank", [P, P], F32)
    count_edges(m, BY_DST, next_rank)
    count_edges(m, BY_SRC, next_rank)

    def start(v):
        v.results_free()
        v.give()
        v.made()
        for tiles, part in pieces(v, 0):
            last = v.dve.tensor_copy(v.buf["h"][:, tiles, :], part)
        v.link(last)
        for row, dst in ((0, v.buf["ssrc"]), (1, v.buf["sdst"])):
            v.link(v.dve.tensor_tensor(v.tmp[:], v.buf["h"][:], across(v.row[row][:], v.NB), ALU.mult))
            v.link(v.dve.tensor_reduce(dst[:, :, 0:H], split_heads(v.tmp[:]), AX_X, ALU.add))
    node_stage(m, "n0", start, [times(0, 0)], weights=[a["W"]], rows=[a["src_attn"], a["dst_attn"]],
               turned_in=a["xT"], buffers=[("h", D), ("ssrc", H + 1), ("sdst", H + 1)],
               stores=[(m.t_ssrc, 0, H, "ssrc"), (m.t_gat, 0, D, "h"), (m.t_gat, D, D + H, "sdst")],
               scatters=[(m.c_ssrc, BY_SRC, "ssrc"), (m.c_sdst, BY_DST, "sdst")])
    tile_windows(m, BY_DST, m.by_dst())
    sort_by_src(m, next_rank)
    tile_windows(m, BY_SRC, m.by_src())

    guard = nc.cleanup_on_exit()
    guard.__enter__()
    scores = nc.alloc_sbuf_tensor("scores", [P, m.F], F32)
    maxima = nc.alloc_sbuf_tensor("maxima", [P, m.F], F32)

    def gat_score(dve, ch, row, rows, own, rec, tmp, got):
        c = tmp[:, :, 0:H]
        ch.link(dve.tensor_tensor(c, rows, own, ALU.add))
        ch.link(dve.scalar_tensor_tensor(got, c, SLOPE, c, ALU.mult, ALU.max))
    edge_scores(m, m.by_dst(), BY_DST, m.t_ssrc, H, m.c_sdst, "e0", scores, maxima, gat_score)
    run_maxima(m, "m0", scores, maxima, totals=True)
    totals_by_rank(m, "s0", scores, maxima)

    def stats(v):
        v.results_free()
        v.link(v.dve.tensor_scalar(v.buf["none"][:], v.mask[:].unsqueeze(2), -1.0, 1.0, ALU.mult, ALU.add))
        v.link(v.dve.tensor_tensor(v.buf["stat"][:, :, 0:H], v.sums[:, :, D:D + H],
                                   v.buf["none"][:].to_broadcast([P, v.NB, H]), ALU.add))
        v.link(v.dve.reciprocal(v.buf["stat"][:, :, 0:H], v.buf["stat"][:, :, 0:H]))
        v.link(v.dve.tensor_copy(v.buf["stat"][:, :, H:2 * H], v.sums[:, :, D + H:RW]))
    node_stage(m, "n1", stats, [], fetch=BY_DST, cols=slice(D, RW), features=a["x"],
               buffers=[("stat", 2 * H), ("none", 1)], stores=[(m.t_gat, D + H, D + 3 * H, "stat")])
    sum_runs(m, m.by_src(), "s1", GAT)

    def attention_in(v):
        v.results_free()
        v.link(v.dve.tensor_tensor(v.x[:], v.x[:], v.sums[:, :, 0:D], ALU.add))
        normalise(v, v.y[:], v.x[:])
        turned(v)
        v.give()
        v.give()
        v.give()
        v.made()
        add_row(v, v.buf["q"][:, :, 0:D], 2, v.row[0][:])
        v.made()
        add_row(v, v.buf["kv"][:, :, 0:D], 4, v.row[1][:])
        v.made()
        add_row(v, v.buf["kv"][:, :, D:2 * D], 6, v.row[2][:])
    node_stage(m, "n2", attention_in, [turn_into("y", 0), times(0, 2), times(1, 4), times(2, 6)], [root],
               fetch=BY_SRC, cols=slice(0, D), features=a["x"], weights=[a["Wq"], a["Wk"], a["Wv"]],
               rows=[a["bq"], a["bk"], a["bv"]], buffers=[("q", D + 1), ("kv", 2 * D)],
               stores=[(m.x_now, 0, D, "y"), (m.t_kv, 0, 2 * D, "kv")], scatters=[(m.c_q, BY_SRC, "q")])

    def attention_score(dve, ch, row, kv, own, rec, tmp, got):
        ch.link(dve.tensor_tensor(tmp[:], own, kv[:, :, 0:D], ALU.mult))
        ch.link(dve.tensor_reduce(got.rearrange("p t h -> p (t h)"), by_head(tmp[:]), AX_X, ALU.add))
        ch.link(dve.scalar_tensor_tensor(got, got, float(HD) ** -0.5, rec[:, :, 2:SREC].bitcast(F32),
                                         ALU.mult, ALU.mult))
    edge_scores(m, m.by_src(), BY_SRC, m.t_kv, 2 * D, m.c_q, "e1", scores, maxima, attention_score,
                spill_from=D)
    run_maxima(m, "m1", scores, maxima)
    sum_runs(m, m.by_src(), "s2", SOFT, scores, maxima)

    def attention_out(v):
        dve, link = v.dve, v.link
        v.results_free()
        w = v.sums[:, :, D:D + H]
        link(dve.tensor_scalar(w, w, 1e-16, None, ALU.add))
        link(dve.tensor_scalar(v.buf["own"][:], w, 1e-37, None, ALU.max))
        link(dve.reciprocal(v.buf["own"][:], v.buf["own"][:]))
        for t in range(v.NB):
            last = dve.tensor_tensor(v.y[:, t, :].rearrange("p (h c) -> p h c", h=H),
                                     v.sums[:, t, 0:D].rearrange("p (h c) -> p h c", h=H),
                                     wide(v.buf["own"][:, t, :], HD), ALU.mult)
        link(last)
        turned(v)
        v.give()
        v.made()
        add_row(v, v.buf["xl"], 2, v.row[0][:])
        normalise(v, v.y[:], v.buf["xl"][:])
        link(dve.tensor_tensor(v.y[:], v.y[:], across(v.row[1][:], v.NB), ALU.mult))
        link(dve.tensor_tensor(v.y[:], v.y[:], across(v.row[2][:], v.NB), ALU.add))
        link(dve.scalar_tensor_tensor(v.x[:], v.x[:], 2.0, v.y[:], ALU.mult, ALU.add))
        normalise(v, v.y[:], v.x[:])
        turned(v)
        v.give()
        v.give()
        v.made()
        for tiles, part in pieces(v, 4):
            last = dve.tensor_copy(v.buf["xl"][:, tiles, :], part)
        link(last)
        v.made()
        for tiles, part in pieces(v, 6):
            last = dve.tensor_copy(v.buf["xr"][:, tiles, 0:D], part)
        link(last)
        link(dve.tensor_tensor(v.tmp[:], v.buf["xl"][:], v.buf["xr"][:, :, 0:D], ALU.add))
        link(dve.scalar_tensor_tensor(v.tmp[:], v.tmp[:], SLOPE, v.tmp[:], ALU.mult, ALU.max))
        link(dve.tensor_tensor(v.tmp[:], v.tmp[:], across(v.row[3][:], v.NB), ALU.mult))
        link(dve.tensor_reduce(flat_heads(v.buf["own"][:]), by_head(v.tmp[:]), AX_X, ALU.add))
    node_stage(m, "n3", attention_out,
               [turn_into("y", 0), times(0, 2), turn_into("y", 0), times(1, 4), times(2, 6)], [root, root],
               fetch=BY_SRC, cols=slice(0, RW), weights=[a["Wo"], a["Wl"], a["Wr"]],
               rows=[a["bo"], a["gamma"], a["beta"], a["att"]],
               buffers=[("own", H), ("xl", D), ("xr", D + 1)],
               stores=[(m.x_now, 0, D, "y"), (m.t_xl, 0, D, "xl"), (m.t_own, 0, H, "own")],
               scatters=[(m.c_xr, BY_DST, "xr")])

    def gatv2_score(dve, ch, row, rows, own, rec, tmp, got):
        t = tmp[:]
        ch.link(dve.tensor_tensor(t, rows, own, ALU.add))
        ch.link(dve.scalar_tensor_tensor(t, t, SLOPE, t, ALU.mult, ALU.max))
        ch.link(dve.tensor_tensor(t, t, across(row[0][:], STEP), ALU.mult))
        ch.link(dve.tensor_reduce(got.rearrange("p t h -> p (t h)"), by_head(t), AX_X, ALU.add))
    edge_scores(m, m.by_dst(), BY_DST, m.t_xl, D, m.c_xr, "e2", scores, maxima, gatv2_score, spill_from=0,
                rows=[a["att"]])
    run_maxima(m, "m2", scores, maxima)
    sum_runs(m, m.by_dst(), "s3", SOFT, scores, maxima)
    guard.__exit__(None, None, None)
    nc.all_engine_barrier()

    def gatv2_out(v):
        dve, link = v.dve, v.link
        v.results_free()
        e = v.buf["e"]
        mx = v.sums[:, :, D + H:RW]
        link(dve.tensor_scalar(v.small[:, 0, :], v.mask[:], -LOW, LOW, ALU.mult, ALU.add))
        link(dve.tensor_tensor(mx, mx, wide(v.small[:, 0, :], H), ALU.add))
        link(dve.tensor_tensor(e[:, :, 2 * H:3 * H], mx, v.buf["own"][:], ALU.max))
        link(dve.tensor_tensor(e[:, :, 0:H], mx, e[:, :, 2 * H:3 * H], ALU.subtract))
        link(dve.tensor_tensor(e[:, :, H:2 * H], v.buf["own"][:], e[:, :, 2 * H:3 * H], ALU.subtract))
        v.ask()
        link(dve.tensor_tensor(e[:, :, 2 * H:3 * H], v.sums[:, :, D:D + H], e[:, :, 0:H], ALU.mult))
        link(dve.tensor_tensor(e[:, :, 2 * H:3 * H], e[:, :, 2 * H:3 * H], e[:, :, H:2 * H], ALU.add))
        link(dve.reciprocal(e[:, :, 2 * H:3 * H], e[:, :, 2 * H:3 * H]))
        link(dve.tensor_tensor(e[:, :, 0:H], e[:, :, 0:H], e[:, :, 2 * H:3 * H], ALU.mult))
        link(dve.tensor_tensor(e[:, :, H:2 * H], e[:, :, H:2 * H], e[:, :, 2 * H:3 * H], ALU.mult))
        for src, k, dst in ((v.sums, 0, v.y), (v.buf["xl"], 1, v.tmp)):
            for t in range(v.NB):
                last = dve.tensor_tensor(dst[:, t, :].rearrange("p (h c) -> p h c", h=H),
                                         src[:, t, 0:D].rearrange("p (h c) -> p h c", h=H),
                                         wide(e[:, t, k * H:(k + 1) * H], HD), ALU.mult)
            link(last)
        link(dve.tensor_tensor(v.y[:], v.y[:], v.tmp[:], ALU.add))
        link(dve.tensor_tensor(v.y[:], v.y[:], across(v.row[0][:], v.NB), ALU.add))
        link(dve.tensor_scalar(v.tmp[:], v.y[:], 0.0, None, ALU.min))
        v.ask()
        link(dve.tensor_scalar(v.y[:], v.y[:], 0.0, -1.0, ALU.max, ALU.add))
        link(dve.tensor_tensor(v.y[:], v.y[:], v.tmp[:], ALU.add))
        link(dve.tensor_tensor(v.x[:], v.x[:], v.y[:], ALU.add))
        normalise(v, v.y[:], v.x[:])
        turned(v)
        v.give()
        v.made()
        for tiles, part in pieces(v, 2):
            last = dve.tensor_copy(v.buf["h"][:, tiles, :], part)
        link(last)

    def exp_e(v, act):
        return act.activation(v.buf["e"][:, :, 0:2 * H], v.buf["e"][:, :, 0:2 * H], ACT.Exp)

    def exp_tmp(v, act):
        return act.activation(v.tmp[:], v.tmp[:], ACT.Exp)
    node_stage(m, "n4", gatv2_out, [turn_into("y", 0), times(0, 2)], [exp_e, exp_tmp, root],
               fetch=BY_DST, cols=slice(0, RW), weights=[a["W_in"]], rows=[a["bias"]],
               buffers=[("own", H), ("xl", D), ("e", 3 * H), ("h", D)],
               stores=[(m.x_now, 0, D, "y"), (m.t_h3, 0, D, "h")],
               also=[("own", m.t_own), ("xl", m.t_xl)])

    sum_runs(m, m.by_dst(), "s4", FILTER)

    def last_layer(v):
        dve, link = v.dve, v.link
        v.results_free()
        link(dve.tensor_copy(v.y[:], v.sums[:, :, 0:D]))
        turned(v)
        v.give()
        v.made()
        add_row(v, v.y, 2, v.row[0][:])
        v.ask()
        turned(v)
        v.give()
        v.made()
        add_row(v, v.y, 2, v.row[1][:])
        link(dve.tensor_tensor(v.x[:], v.x[:], v.y[:], ALU.add))
        normalise(v, v.y[:], v.x[:])

    def tanh_y(v, act):
        return act.activation(v.y[:], v.y[:], ACT.Tanh)
    node_stage(m, "n5", last_layer, [turn_into("y", 0), times(0, 2), turn_into("y", 0), times(1, 2)],
               [tanh_y, root], fetch=BY_DST, cols=slice(0, D), weights=[a["W_out"], a["W_lin"]],
               rows=[a["b_out"], a["b_lin"]], stores=[(out, 0, D, "y")])



def kernel(**inputs):
    import concourse.bacc as bacc
    from concourse.bass_utils import run_bass_kernel_spmd

    x = np.asarray(inputs["x"])
    src, dst = np.asarray(inputs["src"]), np.asarray(inputs["dst"])
    N, E = x.shape[0], src.shape[0]
    G = -(-E // (P * CHUNKS))
    T = CHUNKS * G
    NB = 7
    NT = -(-(-(-(N + 1) // P)) // NB) * NB

    def pad(a, n, value=0):
        return np.concatenate([a, np.full((n - a.shape[0], *a.shape[1:]), value, a.dtype)])

    def tiled(a):
        a = a.reshape(CHUNKS, G, P, *a.shape[1:])
        return np.ascontiguousarray(a.transpose(2, 1, 0, *range(3, a.ndim)))

    rec = np.stack([pad(src, T * P, N), pad(dst, T * P, N)], axis=1)
    attr = pad(np.asarray(inputs["edge_attr_50"]), T * P).reshape(CHUNKS, G, P, -1)
    xp = pad(x, NT * P)
    arrays = {
        "x": xp, "xT": np.ascontiguousarray(xp.T),
        "rec_by_dst": tiled(rec).reshape(P, T * 2),
        "edge_attr_8": tiled(pad(np.asarray(inputs["edge_attr_8"]), T * P)).reshape(P, T * H),
        "edge_weight": tiled(pad(np.asarray(inputs["edge_weight"]), T * P)).reshape(P, T),
        "edge_attr_50": np.ascontiguousarray(attr.transpose(3, 1, 0, 2)).reshape(-1, T * P),
        "src_attn": np.asarray(inputs["L0_gnn_src_attn"]).reshape(-1),
        "dst_attn": np.asarray(inputs["L0_gnn_dst_attn"]).reshape(-1),
        "att": np.asarray(inputs["L2_gnn_att"]).reshape(-1),
        "W": inputs["L0_gnn_W"],
    }
    for name in ("Wq", "bq", "Wk", "bk", "Wv", "bv", "Wo", "bo", "gamma", "beta"):
        arrays[name] = inputs[f"L1_gnn_{name}"]
    for name in ("Wl", "Wr", "bias"):
        arrays[name] = inputs[f"L2_gnn_{name}"]
    for name in ("W_f1", "b_f1", "W_f2", "b_f2", "W_in", "W_out", "b_out", "W_lin", "b_lin"):
        arrays[name] = inputs[f"L3_gnn_{name}"]
    arrays = {f"in_{k}": np.ascontiguousarray(v) for k, v in arrays.items()}

    nc = bacc.Bacc("TRN2", target_bir_lowering=False, num_devices=1)
    args = {k[3:]: nc.dram_tensor(k, v.shape, mybir.dt.from_np(v.dtype), kind="ExternalInput").ap()
            for k, v in arrays.items()}
    out = nc.dram_tensor("out", (NT * P, D), F32, kind="ExternalOutput").ap()
    build(nc, args, out, N, G, NB)
    r = run_bass_kernel_spmd(nc, [arrays], core_ids=[0])
    return r.results[0]["out"][:N]
```
